# Optimizing a Trainium2 kernel written in Bass

```python
import numpy as np
import jax
import jax.numpy as jnp

def _softmax(x, axis=-1):
    return jax.nn.softmax(x, axis=axis)

def _gelu(x):
    return jax.nn.gelu(x, approximate=True)

def _silu(x):
    return jax.nn.silu(x)

def _sigmoid(x):
    return jax.nn.sigmoid(x)

def _layernorm(x, axis=-1, eps=1e-05):
    m = jnp.mean(x, axis=axis, keepdims=True)
    v = jnp.var(x, axis=axis, keepdims=True)
    return (x - m) / jnp.sqrt(v + eps)

def _scatter_add(tgt, idx, src, axis=0):
    return tgt.at[idx].add(src)

def _segment_sum(src, seg, n):
    return jax.ops.segment_sum(src, seg, n)
kernel_name = 'mk_decoder_preln_d1_seqx_r4_de07c7'

def setup_inputs(seed: int=0):
    np.random.seed(seed)
    _w = jnp.asarray

    def _rec_inputs():
        import jax
        import jax.numpy as jnp
        _rk = jax.random.key(seed)
        x = -0.0002928 + 1 * jax.random.normal(jax.random.fold_in(_rk, 1), (8, 512, 256), jnp.float32)
        _lenS = 512 - jax.random.randint(jax.random.fold_in(_rk, 7), (8,), 0, max(1, 512 // 4) + 1, jnp.int32)
        _lenS2 = 512 - jax.random.randint(jax.random.fold_in(_rk, 8), (8,), 0, max(1, 512 // 4) + 1, jnp.int32)
        _ctx_1024P = jax.random.normal(jax.random.fold_in(_rk, 11), (8, 16, 256), jnp.float32)
        _ctx_1024c = jax.random.dirichlet(jax.random.fold_in(_rk, 511), 0.3 * jnp.ones((16,), jnp.float32), (8, 512))
        _ctx_1024t = jnp.einsum('bsk,bkd->bsd', _ctx_1024c, _ctx_1024P)
        _ctx_1024t = _ctx_1024t * jax.lax.rsqrt(jnp.mean(jnp.square(_ctx_1024t)) + 1e-12) * 0.953939
        ctx_1024 = -1.39393e-06 + 0.999914 * (_ctx_1024t + 0.3 * jax.random.normal(jax.random.fold_in(_rk, 611), (8, 512, 256), jnp.float32))
        return (x, ctx_1024)
    x, ctx_1024 = _rec_inputs()

    def _L0_attn_setup():
        import jax, jax.numpy as jnp
        import numpy as np
        D_MODEL = 256
        N_HEADS = 16
        HEAD_DIM = D_MODEL // N_HEADS

        def alibi_slopes(n_heads):
            base = 2.0 ** (-8.0 / n_heads)
            return jnp.asarray([base ** i for i in range(1, n_heads + 1)], dtype=jnp.float32)
        key = jax.random.key(seed)
        kx, kq, kk, kv, ko = jax.random.split(key, 5)
        B, T = (2, 512)
        scale = 0.02
        x = jax.random.normal(kx, (B, T, D_MODEL), dtype=jnp.float32)
        Wq = jax.random.normal(kq, (D_MODEL, D_MODEL), dtype=jnp.float32) * scale
        Wk = jax.random.normal(kk, (D_MODEL, D_MODEL), dtype=jnp.float32) * scale
        Wv = jax.random.normal(kv, (D_MODEL, D_MODEL), dtype=jnp.float32) * scale
        Wo = jax.random.normal(ko, (D_MODEL, D_MODEL), dtype=jnp.float32) * scale
        return {'x': x, 'Wq': Wq, 'Wk': Wk, 'Wv': Wv, 'Wo': Wo}
    _L0_attn_all = _L0_attn_setup()
    _L0_attn_in = {k: v for k, v in _L0_attn_all.items() if k in ('Wq', 'Wk', 'Wv', 'Wo')}
    del _L0_attn_all

    def _L0_xattn_setup():
        import jax, jax.numpy as jnp
        import numpy as np
        HEADS = 16
        key = jax.random.key(seed)
        k1, k2, k3 = jax.random.split(key, 3)
        B, S, D = (2, 512, 256)
        return {'query': jax.random.normal(k1, (B, S, D), dtype=jnp.float32), 'key': jax.random.normal(k2, (B, S, D), dtype=jnp.float32), 'value': jax.random.normal(k3, (B, S, D), dtype=jnp.float32)}
    _L0_xattn_all = _L0_xattn_setup()
    _L0_xattn_in = {k: v for k, v in _L0_xattn_all.items() if k in ()}
    del _L0_xattn_all

    def _L0_ffn_setup():
        import jax, jax.numpy as jnp
        import numpy as np
        DIM = 256
        HIDDEN = 768
        SCALE = 1.0 / 127.0

        def _dequant(w_int, dtype):
            return w_int.astype(dtype) * jnp.asarray(SCALE, dtype)
        key = jax.random.key(seed)
        k_x, k_g, k_u, k_d = jax.random.split(key, 4)
        x = jax.random.normal(k_x, (4, 512, DIM), dtype=jnp.float32)
        w_gate = jax.random.randint(k_g, (HIDDEN, DIM), -127, 128, dtype=jnp.int32)
        w_up = jax.random.randint(k_u, (HIDDEN, DIM), -127, 128, dtype=jnp.int32)
        w_down = jax.random.randint(k_d, (DIM, HIDDEN), -127, 128, dtype=jnp.int32)
        return {'x': x, 'w_gate': w_gate, 'w_up': w_up, 'w_down': w_down}
    _L0_ffn_all = _L0_ffn_setup()
    _L0_ffn_in = {k: v for k, v in _L0_ffn_all.items() if k in ('w_gate', 'w_up', 'w_down')}
    del _L0_ffn_all
    return {'x': x, 'ctx_1024': ctx_1024, 'L0_attn_Wq': _L0_attn_in['Wq'], 'L0_attn_Wk': _L0_attn_in['Wk'], 'L0_attn_Wv': _L0_attn_in['Wv'], 'L0_attn_Wo': _L0_attn_in['Wo'], 'L0_ffn_w_gate': _L0_ffn_in['w_gate'], 'L0_ffn_w_up': _L0_ffn_in['w_up'], 'L0_ffn_w_down': _L0_ffn_in['w_down']}

def reference(x, ctx_1024, L0_attn_Wq, L0_attn_Wk, L0_attn_Wv, L0_attn_Wo, L0_ffn_w_gate, L0_ffn_w_up, L0_ffn_w_down):
    import jax
    import jax.numpy as jnp

    def _L0_attn_ref(x, Wq, Wk, Wv, Wo):
        import jax, jax.numpy as jnp
        import numpy as np
        D_MODEL = 256
        N_HEADS = 16
        HEAD_DIM = D_MODEL // N_HEADS

        def alibi_slopes(n_heads):
            base = 2.0 ** (-8.0 / n_heads)
            return jnp.asarray([base ** i for i in range(1, n_heads + 1)], dtype=jnp.float32)
        B, T, D = x.shape
        H, hd = (N_HEADS, HEAD_DIM)

        def proj(W):
            return (x @ W.T).reshape(B, T, H, hd).transpose(0, 2, 1, 3)
        q, k, v = (proj(Wq), proj(Wk), proj(Wv))
        scale = hd ** (-0.5)
        scores = jnp.einsum('bhqd,bhkd->bhqk', q, k) * scale
        pos = jnp.arange(T, dtype=jnp.float32)
        dist = jnp.abs(pos[:, None] - pos[None, :])
        causal = pos[:, None] >= pos[None, :]
        slopes = alibi_slopes(H)
        bias = -slopes[:, None, None] * jnp.where(causal, dist, 0.0)
        scores = scores + bias[None]
        scores = jnp.where(causal[None, None], scores, -jnp.inf)
        attn = jax.nn.softmax(scores, axis=-1)
        out = jnp.einsum('bhqk,bhkd->bhqd', attn, v)
        out = out.transpose(0, 2, 1, 3).reshape(B, T, D)
        return out @ Wo.T

    def _L0_xattn_ref(query, key, value):
        import jax, jax.numpy as jnp
        import numpy as np
        HEADS = 16
        B, S, D = query.shape
        H = HEADS
        dh = D // H
        q = query.reshape(B, S, H, dh)
        k = key.reshape(B, S, H, dh)
        v = value.reshape(B, S, H, dh)
        scale = 1.0 / jnp.sqrt(jnp.asarray(dh, dtype=query.dtype))
        scores = jnp.einsum('bqhd,bkhd->bhqk', q, k) * scale
        probs = jax.nn.softmax(scores, axis=-1)
        out = jnp.einsum('bhqk,bkhd->bqhd', probs, v)
        return out.reshape(B, S, D)

    def _L0_ffn_ref(x, w_gate, w_up, w_down):
        import jax, jax.numpy as jnp
        import numpy as np
        DIM = 256
        HIDDEN = 768
        SCALE = 1.0 / 127.0

        def _dequant(w_int, dtype):
            return w_int.astype(dtype) * jnp.asarray(SCALE, dtype)
        wg = _dequant(w_gate, x.dtype)
        wu = _dequant(w_up, x.dtype)
        wd = _dequant(w_down, x.dtype)
        gate = jnp.einsum('bsd,hd->bsh', x, wg)
        up = jnp.einsum('bsd,hd->bsh', x, wu)
        h = jax.nn.silu(gate) * up
        return jnp.einsum('bsh,dh->bsd', h, wd)
    x = x + _L0_attn_ref(_layernorm(x, axis=-1), L0_attn_Wq, L0_attn_Wk, L0_attn_Wv, L0_attn_Wo)
    x = x + _L0_xattn_ref(_layernorm(x, axis=-1), ctx_1024, ctx_1024)
    x = x + _L0_ffn_ref(_layernorm(x, axis=-1), L0_ffn_w_gate, L0_ffn_w_up, L0_ffn_w_down)
    return x

_drawn_inputs = setup_inputs


def setup_inputs(seed=0):
    import zlib

    import numpy as np

    out = dict(_drawn_inputs(seed))
    spreads = {}
    factors = {'L0_attn_Wq': 8.0, 'L0_attn_Wk': 8.0}
    for name, (base, spread) in spreads.items():
        noise = np.random.default_rng([zlib.crc32(name.encode()), seed]).standard_normal(out[name].shape)
        drawn = base * np.exp(spread * noise) if base else spread * noise
        out[name] = jnp.asarray(drawn.astype(out[name].dtype))
    for name, factor in factors.items():
        out[name] = (out[name] * factor).astype(out[name].dtype)
    return out
```

```python
import concourse.bass as bass
from concourse import mybir
from contextlib import ExitStack


def decoder_kernel(nc, x, ctx, wq, wk, wv, wo, w_gate, w_up, w_down, ramp, fill, masks, parts_dram, out):
    f32, bf16 = mybir.dt.float32, mybir.dt.bfloat16
    ALU, ACT, AX = mybir.AluOpType, mybir.ActivationFunctionType, mybir.AxisListType

    B, T, D = x.shape
    HD = 16
    NH = D // HD
    HID = w_gate.shape[1]
    NT = T // 128
    KC = D // 128
    NHID = HID // 128
    NG = 4
    GH = NH // NG
    HH = NH // 2
    QP = [0, 0, 1, 1, 0, 2]
    KP = [0, 1, 0, 1, 2, 0]
    R_MAX = 16 * len(QP) + 3
    R_ALL = R_MAX + 3
    S, X = 0, 1
    QS, KS, KX, QX = 0, 1, 2, 3
    SCALE = HD ** -0.5
    EPS = 1e-5
    LAST = B - 1

    def width(u, kt):
        return T - 128 * kt if u == S else T

    def chunks(u, kt):
        n = 4 if u == S and kt >= 2 else 2
        return [list(range(i, i + n)) for i in range(0, GH, n)]

    EXPS = [sum(len(chunks(u, kt)) for kt in range(NT)) for u in (S, X)]
    E_ALL = NG * sum(EXPS)

    def job(u, t, g):
        return 2 * NG * t + NG * u + g

    def exp_no(u, t, g, c):
        return E_ALL * t + NG * EXPS[S] * u + EXPS[u] * g + c

    def max_no(u, t, g, i):
        return 2 * NH * NT * t + NH * NT * u + GH * NT * g + i

    SPLIT_PLACE = {(QS, 0): 0, (KS, 0): 1, (QS, 1): 2, (KS, 1): 3, (KX, 0): 4, (KX, 1): 5, (QX, 0): 6, (QX, 1): 7}

    def split_no(w, m, t):
        return 8 * t + SPLIT_PLACE[w, m]

    BESIDE = {
        (X, 0): [["mt"], ["xt0_n"], ["xt1_n"], ["qs0_n"]],
        (X, 1): [["mt", "ks0_n"], ["ot", "qs1_n"], ["ks1_n"], ["v0_n", "v1_n"]],
        (X, 2): [["mt"], ["ot"], [], []],
        (X, 3): [["mt"], ["ot"], [], []],
        (S, 0): [["mt"], ["ot"], [], []],
        (S, 1): [["mt"], ["ot"], [], []],
        (S, 2): [["mt"], ["ot"], ["kx0"], ["kx1"]],
        (S, 3): [["yt0_p"], ["ot"], ["yt1_p"], []],
    }

    es = ExitStack()
    with es:
        def sb(name, shape, dt=f32):
            return es.enter_context(nc.sbuf_tensor(name, shape, dt))

        def sem(name):
            return es.enter_context(nc.semaphore(name))

        LQ = [sb("lq_self", [128, NH, T], bf16), sb("lq_cross", [128, NH, T], bf16)]
        LK = [sb("lk_self", [128, NH, T], bf16), sb("lk_cross", [128, NH, T], bf16)]
        V = [sb("v_self", [128, NT, NH, 2 * HD]), sb("v_cross", [128, NT, NH, 2 * HD])]
        P = [sb(f"probs{i}", [128, GH, T]) for i in range(2)]
        x_in = sb("x_in", [128, NT, D])
        ctx_in = sb("ctx_in", [128, NT, D])
        x1 = sb("x1", [128, NT, D])
        x2 = sb("x2", [128, NT, D])
        att = sb("att", [128, NT, D])
        ln = sb("ln", [128, NT, D])
        xT = sb("xT", [128, KC, T])
        yT = sb("yT", [128, KC, T])
        oT = sb("oT", [128, KC, T])
        hid = sb("hid", [128, NHID, T])
        y_out = sb("y_out", [128, NT, D])
        parts = [sb(f"parts{i}", [128, 3, T], bf16) for i in range(2)]
        rest = [sb(f"rest{i}", [128, T]) for i in range(2)]
        pv_sb = sb("pv_sb", [128, T])
        mx = [sb(f"mx{i}", [128, NT, GH]) for i in range(2)]
        mxr = [sb(f"mxr{i}", [128, 2, NT, GH]) for i in range(2)]
        mxp = [sb(f"mxp{i}", [128, NT, 3, GH], bf16) for i in range(2)]
        mT = [sb(f"mT{i}", [3 * GH, T], bf16) for i in range(2)]
        rden = [sb(f"rden{i}", [128, NT, GH]) for i in range(2)]
        stats = sb("stats", [128, NT, 6])
        mv = sb("mv", [128, NT, 2])
        var_eps = sb("var_eps", [128, NT])
        rstd = sb("rstd", [128, NT])
        mhalf = sb("mhalf", [128, NT])
        ident = sb("ident", [128, 128])
        identb = sb("identb", [128, 128], bf16)
        maskb = sb("maskb", [128, 2, 128], bf16)
        Wq, Wk, Wv, Wo = (sb(f"w{n}_sb", [128, KC, D]) for n in "qkvo")
        Wg, Wu = sb("wg_sb", [128, KC, HID]), sb("wu_sb", [128, KC, HID])
        Wd = sb("wd_sb", [128, NHID, D])
        i32 = mybir.dt.int32
        wg_i = P[0][:, :, :].rearrange("p h t -> p (h t)").bitcast(i32)[:, 0:KC * HID]
        wu_i = P[1][:, :, :].rearrange("p h t -> p (h t)").bitcast(i32)[:, 0:KC * HID]
        wd_i = hid[:, :, :].rearrange("p h t -> p (h t)").bitcast(i32)[:, 0:NHID * D]

        score_ps = [es.enter_context(nc.psum_tensor(f"score_ps{i}", [128, 2, 512], f32)) for i in range(2)]
        max_ps = [es.enter_context(nc.psum_tensor(f"max_ps{i}", [128, 512], f32)) for i in range(2)]
        pv_ps = es.enter_context(nc.psum_tensor("pv_ps", [128, 512], f32))
        side = es.enter_context(nc.psum_tensor("side", [128, 512], f32))
        sideb = side[:, :].bitcast(bf16)

        s_const, s_w, s_wi, s_x, s_ctx, s_out = (sem(n) for n in ("const_in", "w_in", "wi_in", "x_in", "ctx_in", "out"))
        s_parts_out = sem("parts_out")
        s_rows = [[sem(f"rows_{u}{m}") for m in range(2)] for u in "sx"]
        s_mrow = [sem(f"mrow{i}") for i in range(2)]
        s_carry = sem("carries_waits")
        s_set, s_ident, s_gw = sem("set"), sem("identity"), sem("ffn_w")
        s_max_ps, s_max = sem("max_ps"), sem("max_taken")
        s_mpart, s_mt_ps, s_mt = sem("max_parts"), sem("mt_ps"), sem("mt_taken")
        s_score, s_exp, s_pv, s_pvout = sem("score_ps"), sem("exp"), sem("pv_ps"), sem("pv_taken")
        s_ot_ps, s_rden, s_ot = sem("ot_ps"), sem("rden"), sem("ot_taken")
        s_sp_ps, s_hi, s_rest, s_mid, s_lo = (sem(n) for n in ("split_ps", "part_hi", "part_rest", "part_mid", "part_lo"))
        s_stat, s_aggr, s_vare, s_rstd, s_ln = ([sem(f"{n}{i}") for i in range(3)]
                                               for n in ("ln_stat", "ln_aggr", "ln_vare", "ln_rstd", "ln_done"))
        s_xt_ps, s_xt, s_yt_ps, s_yt = sem("xt_ps"), sem("xt_taken"), sem("yt_ps"), sem("yt_taken")
        s_v_ps, s_v, s_vx = sem("v_ps"), sem("v_taken"), sem("v_cross")
        s_att_ps, s_att, s_wo_ps, s_x1, s_x2 = (sem(n) for n in ("attT_ps", "attT_taken", "wo_ps", "x1", "x2"))
        s_gu_ps, s_silu, s_hid, s_dn_ps, s_y = (sem(n) for n in ("gu_ps", "silu", "hidden", "down_ps", "y"))

        block = es.enter_context(nc.Block())

        def wait_apart(engine, semaphore, value):
            engine.wait_ge(semaphore, value)
            engine.sem_inc(s_carry, 1)

        def tag(item, t):
            if item.endswith("_n"):
                return t + 1, item[:-2]
            if item.endswith("_p"):
                return t - 1, item[:-2]
            return t, item

        def beside(u, g, kt, t, whole):
            for item in BESIDE[u, g][kt]:
                if whole == "first" and item.endswith("_p") or whole == "last" and item.endswith("_n"):
                    continue
                if item == "ot" and (u, g) == (S, 0) and whole == "first":
                    continue
                if item == "mt" and (u, g) == (X, 3) and whole == "last":
                    continue
                tt, name = tag(item, t)
                yield name, tt

        def next_job(u, t, g):
            return (u, t, g + 1) if g < NG - 1 else (1 - u, t + u, 0)

        def prev_job(u, t, g):
            return (u, t, g - 1) if g else (1 - u, t - 1 + u, NG - 1)

        def max_job(u, t, g, whole):
            if g < 2:
                return u, t, g + 2
            if u == X and whole != "last":
                return S, t + 1, g - 2
            return None

        @block.sync
        def _(sp):
            def load_x(t):
                if not isinstance(t, int) or t > 0:
                    sp.wait_ge(s_x1, NT // 2 * t)
                sp.dma_start(x_in[:, :, :], x[t, :, :].rearrange("(c p) d -> p c d", p=128)).then_inc(s_x, 16)

            def load_ctx(t):
                if not isinstance(t, int) or t > 0:
                    sp.wait_ge(s_sp_ps, 8 * t - 2)
                    sp.wait_ge(s_vx, t)
                sp.dma_start(ctx_in[:, :, :], ctx[t, :, :].rearrange("(c p) d -> p c d", p=128)).then_inc(s_ctx, 16)

            def split(w, m, t):
                n = split_no(w, m, t)
                sp.wait_ge(s_lo, n + 1)
                sp.dma_start(parts_dram[w, :, 128 * m:128 * m + 128, :].rearrange("a p c -> p a c"),
                             parts[SPLIT_PLACE[w, m] % 2][:, :, :]).then_inc(s_parts_out, 16)
                sp.wait_ge(s_parts_out, 16 * n + 16)
                u = S if w in (QS, KS) else X
                rows, order = (LQ[u], QP) if w in (QS, QX) else (LK[u], KP)
                for b, part in enumerate(order):
                    sp.dma_start(rows[16 * b:16 * b + 16, HH * m:HH * m + HH, :],
                                 parts_dram[w, part, 128 * m:128 * m + 128, :].rearrange("(h d) c -> d h c", d=HD)
                                 ).then_inc(s_rows[u][m], 16)

            def store(t):
                sp.wait_ge(s_y, NT // 2 * (t + 1))
                sp.dma_start(out[t, :, :].rearrange("(c p) d -> p c d", p=128), y_out[:, :, :]).then_inc(s_out, 16)

            sp.dma_start(x_in[:, :, :], x[0, :, :].rearrange("(c p) d -> p c d", p=128)).then_inc(s_x, 16)
            sp.dma_start(maskb[:, :, :], masks[:, 0:2, :]).then_inc(s_const, 16)
            sp.dma_start(identb[:, :], masks[:, 2, :]).then_inc(s_const, 16)
            for w_sb, w in ((Wq, wq), (Wk, wk), (Wv, wv), (Wo, wo)):
                sp.dma_start(w_sb[:, :, :], w.rearrange("(c p) n -> p c n", p=128)).then_inc(s_w, 16)
            for u in (S, X):
                sp.dma_start(LQ[u][R_MAX - 3:R_MAX, :, :], fill).then_inc(s_const, 16)
                sp.dma_start(LK[u][R_MAX:R_ALL, :, :], fill).then_inc(s_const, 16)
                sp.dma_start(LK[u][R_MAX - 3:R_MAX, :, :], ramp[u, :, :, :]).then_inc(s_const, 16)
            sp.dma_start(wg_i, w_gate.rearrange("(c p) n -> p c n", p=128)).then_inc(s_wi, 16)
            sp.dma_start(wu_i, w_up.rearrange("(c p) n -> p c n", p=128)).then_inc(s_wi, 16)
            sp.dma_start(wd_i, w_down.rearrange("(c p) n -> p c n", p=128)).then_inc(s_wi, 16)
            load_ctx(0)
            for w, m in ((QS, 0), (KS, 0), (QS, 1), (KS, 1), (KX, 0), (KX, 1), (QX, 0), (QX, 1)):
                split(w, m, 0)

            def body(t):
                load_x(t + 1)
                load_ctx(t + 1)
                for w, m in ((QS, 0), (KS, 0), (QS, 1), (KS, 1), (KX, 0), (KX, 1), (QX, 0), (QX, 1)):
                    split(w, m, t + 1)
                store(t)

            with sp.Fori(0, LAST) as t:
                body(t)
            store(LAST)
            sp.wait_ge(s_out, 16 * B)

        @block.gpsimd
        def _(pool):
            nc.gpsimd.memset(ident[:, :], 0.0).then_inc(s_ident, 1)
            nc.gpsimd.memset(mhalf[:, :], -0.5).then_inc(s_set, 1)
            for u in (S, X):
                nc.gpsimd.memset(V[u][:, :, :, HD:2 * HD], 1.0).then_inc(s_set, 1)
            pool.wait_ge(s_ident, 1)
            nc.gpsimd.affine_select(out=ident[:, :], in_=ident[:, :], compare_op=ALU.not_equal, fill=1.0, base=0,
                                    pattern=[[-1, 128]], channel_multiplier=1).then_inc(s_ident, 1)

            def norm(i, t):
                wait_apart(pool, s_aggr[i], NT * (t + 1))
                nc.gpsimd.tensor_scalar(var_eps[:, :], mv[:, :, 1], EPS, None, ALU.add).then_inc(s_vare[i], 1)
                pool.wait_ge(s_vare[i], t + 1)
                nc.gpsimd.tensor_tensor(rstd[:, :], var_eps[:, :], mhalf[:, :], ALU.pow).then_inc(s_rstd[i], 1)

            def max_parts(u, t, g):
                j, b = job(u, t, g), g % 2
                left = mxr[b]
                wait_apart(pool, s_max, max_no(u, t, g, GH * NT - 1) + 1)
                nc.gpsimd.tensor_copy(mxp[b][:, :, 0, :], mx[b][:, :, :]).then_inc(s_mpart, 1)
                pool.wait_ge(s_mpart, 5 * j + 1)
                nc.gpsimd.tensor_tensor(left[:, 0, :, :], mx[b][:, :, :], mxp[b][:, :, 0, :], ALU.subtract).then_inc(s_mpart, 1)
                wait_apart(pool, s_mpart, 5 * j + 2)
                nc.gpsimd.tensor_copy(mxp[b][:, :, 1, :], left[:, 0, :, :]).then_inc(s_mpart, 1)
                pool.wait_ge(s_mpart, 5 * j + 3)
                nc.gpsimd.tensor_tensor(left[:, 1, :, :], left[:, 0, :, :], mxp[b][:, :, 1, :], ALU.subtract).then_inc(s_mpart, 1)
                wait_apart(pool, s_mpart, 5 * j + 4)
                nc.gpsimd.tensor_copy(mxp[b][:, :, 2, :], left[:, 1, :, :]).then_inc(s_mpart, 1)

            def split(w, m, t):
                n, b = split_no(w, m, t), SPLIT_PLACE[w, m] % 2
                wait_apart(pool, s_rest, n + 1)
                nc.gpsimd.tensor_copy(parts[b][:, 1, :], rest[b][:, :]).then_inc(s_mid, 1)
                pool.wait_ge(s_mid, n + 1)
                nc.gpsimd.tensor_tensor(parts[b][:, 2, :], rest[b][:, :], parts[b][:, 1, :], ALU.subtract).then_inc(s_lo, 1)

            def v_cross(t):
                if not isinstance(t, int) or t > 0:
                    pool.wait_ge(s_pv, NT * job(S, t, 0))
                wait_apart(pool, s_ctx, 16 * (t + 1))
                nc.gpsimd.tensor_copy(V[X][:, :, :, 0:HD],
                                      ctx_in[:, :, :].rearrange("p c (h d) -> p c h d", d=HD)).then_inc(s_vx, 1)

            def add_x2(t):
                pool.wait_ge(s_ot, job(X, t, NG - 1) + 1)
                nc.gpsimd.tensor_tensor(x2[:, :, :], x1[:, :, :], att[:, :, :], ALU.add).then_inc(s_x2, 1)

            def attention(u, t, whole):
                for g in range(NG):
                    for kt in range(NT):
                        for name, tt in beside(u, g, kt, t, whole):
                            if name[:2] in ("qs", "ks", "kx"):
                                split({"qs": QS, "ks": KS, "kx": KX}[name[:2]], int(name[2]), tt)
                        if (u, g, kt) == (X, 0, 0) and whole != "last":
                            norm(0, t + 1)
                        if (u, g, kt) == (S, 0, 1) and whole != "first":
                            add_x2(t - 1)
                        if (u, g, kt) == (S, 0, 2):
                            v_cross(t)
                        if (u, g, kt) == (S, 1, 1) and whole != "first":
                            norm(2, t - 1)
                    ahead = max_job(u, t, g, whole)
                    if ahead:
                        max_parts(*ahead)

            def between(t):
                norm(1, t)
                split(QX, 0, t)
                split(QX, 1, t)
                max_parts(X, t, 0)
                max_parts(X, t, 1)

            pool.wait_ge(s_set, 1)
            norm(0, 0)
            for w, m in ((QS, 0), (KS, 0), (QS, 1), (KS, 1)):
                split(w, m, 0)
            max_parts(S, 0, 0)
            max_parts(S, 0, 1)
            attention(S, 0, "first")
            between(0)
            with pool.Fori(0, LAST) as t:
                attention(X, t, "")
                attention(S, t + 1, "")
                between(t + 1)
            attention(X, LAST, "last")
            add_x2(LAST)
            norm(2, LAST)

        @block.tensor
        def _(pe):
            class Bank:
                def __init__(self):
                    self.free = None

                def take(self, free):
                    if self.free:
                        pe.wait_ge(*self.free)
                    self.free = free

            side_bank, pv_bank = Bank(), Bank()
            score_banks, max_banks = [Bank(), Bank()], [Bank(), Bank()]

            def transpose4(src, m, sem_to, free):
                side_bank.take(free)
                for c in range(NT):
                    last = nc.tensor.transpose(side[:, 128 * c:128 * c + 128], src[:, c, 128 * m:128 * m + 128], ident[:, :])
                last.then_inc(sem_to, 1)

            def project(w_sb, m, t, sem_to, free):
                side_bank.take(free)
                pe.wait_ge(s_xt, KC * (t + 1))
                for k in range(KC):
                    last = nc.tensor.matmul(side[:, :], w_sb[:, k, 128 * m:128 * m + 128], xT[:, k, :],
                                            start=k == 0, stop=k == KC - 1)
                last.then_inc(sem_to, 1)

            def rows_out(w_sb, src, half, sem_to, free):
                side_bank.take(free)
                for c in range(2):
                    r = 2 * half + c
                    for k in range(KC):
                        last = nc.tensor.matmul(side[:, 256 * c:256 * c + 256], src[:, k, 128 * r:128 * r + 128],
                                                w_sb[:, k, :], start=k == 0, stop=k == KC - 1)
                last.then_inc(sem_to, 1)

            def max_transposes(u, t, g):
                j = job(u, t, g)
                side_bank.take((s_mt, j + 1))
                pe.wait_ge(s_mpart, 5 * j + 5)
                for c in range(NT):
                    last = nc.tensor.transpose(sideb[0:3 * GH, 128 * c:128 * c + 128],
                                               mxp[g % 2][:, c, :, :].rearrange("p a h -> p (a h)"), identb[:, :])
                last.then_inc(s_mt_ps, 1)

            def out_transposes(u, t, g):
                j = job(u, t, g)
                side_bank.take((s_ot, j + 1))
                pe.wait_ge(s_pvout, j + 1)
                for c in range(NT):
                    last = nc.tensor.transpose(side[:, 128 * c:128 * c + 128], pv_sb[:, 128 * c:128 * c + 128], ident[:, :])
                last.then_inc(s_ot_ps, 1)

            def side_work(name, t, u, g):
                kind, m = name[:-1], int(name[-1]) if name[-1].isdigit() else 0
                if name == "mt":
                    uu, tt, gg = next_job(u, t, g)
                    max_transposes(uu, tt, gg)
                elif name == "ot":
                    uu, tt, gg = prev_job(u, t, g)
                    out_transposes(uu, tt, gg)
                elif kind == "xt":
                    pe.wait_ge(s_ln[0], NT * (t + 1))
                    transpose4(ln, m, s_xt_ps, (s_xt, KC * t + m + 1))
                elif kind == "yt":
                    pe.wait_ge(s_ln[2], NT * (t + 1))
                    transpose4(ln, m, s_yt_ps, (s_yt, KC * t + m + 1))
                elif kind in ("qs", "ks"):
                    w = QS if kind == "qs" else KS
                    project(Wq if w == QS else Wk, m, t, s_sp_ps, (s_rest, split_no(w, m, t) + 1))
                elif kind == "kx":
                    pe.wait_ge(s_ctx, 16 * (t + 1))
                    transpose4(ctx_in, m, s_sp_ps, (s_rest, split_no(KX, m, t) + 1))
                else:
                    rows_out(Wv, xT, m, s_v_ps, (s_v, 2 * t + m + 1))

            def max_product(u, t, g, i):
                n, b = max_no(u, t, g, i), i % 2
                h, r = GH * g + i // NT, i % NT
                if i == 0 and g % 2 == 0:
                    pe.wait_ge(s_rows[u][g // 2], 16 * 12 * (t + 1))
                max_banks[b].take((s_max, n + 1))
                keys = 128 * (r + 1) if u == S else T
                last = nc.tensor.matmul(max_ps[b][:, 0:keys], LQ[u][0:R_MAX, h, 128 * r:128 * r + 128],
                                        LK[u][0:R_MAX, h, 0:keys], start=True, stop=u == X)
                if u == S:
                    last = nc.tensor.matmul(max_ps[b][:, keys - 128:keys], identb[:, :], maskb[:, 0, :],
                                            start=False, stop=True)
                last.then_inc(s_max_ps, 1)

            def scores(u, t, g, kt, c, heads):
                n = exp_no(u, t, g, sum(len(chunks(u, k)) for k in range(kt)) + c)
                b = (sum(len(chunks(u, k)) for k in range(kt)) + c) % 2
                wd = width(u, kt)
                score_banks[b].take((s_exp, n + 1))
                for i, hh in enumerate(heads):
                    h = GH * g + hh
                    at = i * wd if len(heads) == 4 else i * 512
                    to = score_ps[b][:, :, :].rearrange("p a c -> p (a c)")[:, at:at + wd]
                    last = nc.tensor.matmul(to, LK[u][0:R_ALL, h, 128 * kt:128 * kt + 128],
                                            LQ[u][0:R_ALL, h, T - wd:T], start=True, stop=u == X)
                    if u == S:
                        last = nc.tensor.matmul(to[:, 0:128], identb[:, :], maskb[:, 1, :], start=False, stop=True)
                last.then_inc(s_score, 1)

            def weigh(u, t, g, kt):
                if kt == 0:
                    pv_bank.take((s_pvout, job(u, t, g) + 1))
                pe.wait_ge(s_exp, exp_no(u, t, g, sum(len(chunks(u, k)) for k in range(kt + 1)) - 1) + 1)
                wd = width(u, kt)
                for hh in range(GH):
                    last = nc.tensor.matmul(pv_ps[32 * hh:32 * hh + 32, T - wd:T], V[u][:, kt, GH * g + hh, :],
                                            P[kt % 2][:, hh, 0:wd], start=kt == 0, stop=kt == NT - 1)
                last.then_inc(s_pv, 1)

            def attention(u, t, whole, trailing):
                for g in range(NG):
                    pe.wait_ge(s_mrow[g % 2], 48 * (NG * t + NG // 2 * u + g // 2 + 1))
                    ahead = max_job(u, t, g, whole)
                    for kt in range(NT):
                        if u == S and g == 0 and kt == 0:
                            pe.wait_ge(s_v, 2 * (t + 1))
                        if u == X and g == 0 and kt == 0:
                            pe.wait_ge(s_vx, t + 1)
                        cs = chunks(u, kt)
                        if ahead:
                            max_product(*ahead, 4 * kt)
                        scores(u, t, g, kt, 0, cs[0])
                        if ahead:
                            max_product(*ahead, 4 * kt + 1)
                        if len(cs) > 1:
                            scores(u, t, g, kt, 1, cs[1])
                        if ahead:
                            max_product(*ahead, 4 * kt + 2)
                        if trailing:
                            weigh(*trailing)
                        if ahead:
                            max_product(*ahead, 4 * kt + 3)
                        trailing = (u, t, g, kt)
                        for name, tt in beside(u, g, kt, t, whole):
                            side_work(name, tt if name not in ("mt", "ot") else t, u, g)
                return trailing

            def gate_up(t, i):
                b = i % 2
                score_banks[b].take((s_hid, NHID * t + i + 1))
                for j, w_sb in enumerate((Wg, Wu)):
                    for k in range(KC):
                        last = nc.tensor.matmul(score_ps[b][:, j, :], w_sb[:, k, 128 * i:128 * i + 128], yT[:, k, :],
                                                start=k == 0, stop=k == KC - 1)
                last.then_inc(s_gu_ps, 1)

            def down(t, half, c):
                if c == 0:
                    score_banks[half].take((s_y, 2 * t + half + 1))
                    pe.wait_ge(s_hid, NHID * (t + 1))
                r = 2 * half + c
                for k in range(NHID):
                    last = nc.tensor.matmul(score_ps[half][:, 0, 256 * c:256 * c + 256], hid[:, k, 128 * r:128 * r + 128],
                                            Wd[:, k, :], start=k == 0, stop=k == NHID - 1)
                if c == 1:
                    last.then_inc(s_dn_ps, 1)

            def ffn_start(t):
                pe.wait_ge(s_yt, KC * (t + 1))

            def between(t, whole):
                f = whole != "first"
                weigh(S, t, NG - 1, NT - 1)
                if f:
                    ffn_start(t - 1)
                    gate_up(t - 1, 0)
                out_transposes(S, t, NG - 1)
                if f:
                    gate_up(t - 1, 1)
                for m in range(KC):
                    if m == 0:
                        pe.wait_ge(s_ot, job(S, t, NG - 1) + 1)
                    transpose4(att, m, s_att_ps, (s_att, KC * t + m + 1))
                if f:
                    gate_up(t - 1, 2)
                for half in range(2):
                    if half == 0:
                        pe.wait_ge(s_att, KC * (t + 1))
                    rows_out(Wo, oT, half, s_wo_ps, (s_x1, 2 * t + half + 1))
                if f:
                    gate_up(t - 1, 3)
                    gate_up(t - 1, 4)
                for m in range(KC):
                    if m == 0:
                        pe.wait_ge(s_ln[1], NT * (t + 1))
                    transpose4(ln, m, s_sp_ps, (s_rest, split_no(QX, m, t) + 1))
                if f:
                    gate_up(t - 1, 5)
                    down(t - 1, 0, 0)
                for g in range(2):
                    for q in range(4):
                        for i in range(4):
                            max_product(X, t, g, 4 * q + i)
                        if f and (g, q) in ((0, 0), (0, 2), (1, 0)):
                            down(t - 1, *{(0, 0): (0, 1), (0, 2): (1, 0), (1, 0): (1, 1)}[g, q])
                        if (g, q) == (1, 1):
                            max_transposes(X, t, 0)

            def loop_entry(t):
                side_bank.free = (s_mt, job(X, t, 0) + 1)
                for b in range(2):
                    max_banks[b].free = (s_max, max_no(X, t, 1, GH * NT - 2 + b) + 1)
                pv_bank.free = (s_pvout, job(X, t, 0))

            pe.wait_ge(s_ident, 2)
            pe.wait_ge(s_const, 16 * 8)
            pe.wait_ge(s_w, 16 * 4)
            pe.wait_ge(s_set, 3)
            for name in ("xt0", "xt1", "qs0", "ks0", "qs1", "ks1", "v0", "v1"):
                side_work(name, 0, S, 0)
            for g in range(2):
                for i in range(GH * NT):
                    max_product(S, 0, g, i)
                if g == 0:
                    max_transposes(S, 0, 0)
            trailing = attention(S, 0, "first", None)
            between(0, "first")
            for b in range(2):
                pe.wait_ge(s_exp, exp_no(S, 0, NG - 1, EXPS[S] - 1) + 1)
                score_banks[b].free = None
            pe.wait_ge(s_gw, 3)
            with pe.Fori(0, LAST) as t:
                loop_entry(t)
                trailing = attention(X, t, "", None)
                trailing = attention(S, t + 1, "", trailing)
                between(t + 1, "")
                pe.wait_ge(s_y, 2 * (t + 1))
                score_banks[0].free = score_banks[1].free = None
            loop_entry(LAST)
            for b in range(2):
                score_banks[b].free = None
            trailing = attention(X, LAST, "last", None)
            weigh(*trailing)
            out_transposes(X, LAST, NG - 1)
            for m in range(KC):
                side_work(f"yt{m}", LAST, X, 0)
            ffn_start(LAST)
            for i in range(NHID):
                gate_up(LAST, i)
            for half in range(2):
                for c in range(2):
                    down(LAST, half, c)

        @block.scalar
        def _(act):
            pending = []

            def flush():
                for (u, t, g) in pending:
                    j = job(u, t, g)
                    act.wait_ge(s_mt, j + 1)
                    for a in range(3):
                        act.dma_start(LQ[u][R_MAX + a:R_MAX + a + 1, GH * g:GH * g + GH, :],
                                      mT[g % 2][GH * a:GH * a + GH, :]).then_inc(s_mrow[g % 2], 16)
                pending.clear()

            def max_rows(u, t, g):
                j = job(u, t, g)
                act.wait_ge(s_mt_ps, j + 1)
                nc.scalar.copy(mT[g % 2][:, :], sideb[0:3 * GH, 0:T]).then_inc(s_mt, 1)
                pending.append((u, t, g))

            def pv_out(u, t, g):
                j = job(u, t, g)
                act.wait_ge(s_pv, NT * (j + 1))
                nc.scalar.copy(pv_sb[:, :], pv_ps[:, :]).then_inc(s_pvout, 1)

            def high(w, m, t):
                n, b = split_no(w, m, t), SPLIT_PLACE[w, m] % 2
                act.wait_ge(s_sp_ps, n + 1)
                if SPLIT_PLACE[w, m] >= 2 or not isinstance(t, int) or t > 0:
                    act.wait_ge(s_parts_out, 16 * (n - 1))
                nc.scalar.activation(parts[b][:, 0, :], side[:, :], ACT.Copy,
                                     scale=SCALE if w in (QS, QX) else 1.0).then_inc(s_hi, 1)

            def side_work(name, t, u, g):
                kind, m = name[:-1], int(name[-1]) if name[-1].isdigit() else 0
                if name == "mt":
                    max_rows(*next_job(u, t, g))
                elif kind == "xt":
                    act.wait_ge(s_xt_ps, KC * t + m + 1)
                    nc.scalar.copy(xT[:, m, :], side[:, :]).then_inc(s_xt, 1)
                elif kind == "yt":
                    act.wait_ge(s_yt_ps, KC * t + m + 1)
                    nc.scalar.copy(yT[:, m, :], side[:, :]).then_inc(s_yt, 1)
                elif kind in ("qs", "ks", "kx"):
                    high({"qs": QS, "ks": KS, "kx": KX}[kind], m, t)
                elif kind == "v":
                    act.wait_ge(s_v_ps, 2 * t + m + 1)
                    nc.scalar.copy(V[S][:, 2 * m:2 * m + 2, :, 0:HD],
                                   side[:, :].rearrange("p (c h d) -> p c h d", c=2, d=HD)).then_inc(s_v, 1)

            def attention(u, t, whole, trailing):
                for g in range(NG):
                    c = 0
                    for kt in range(NT):
                        wd = width(u, kt)
                        before = NT * job(u, t, g) + kt - 1
                        if not (isinstance(before, int) and before <= 0):
                            act.wait_ge(s_pv, before)
                        for heads in chunks(u, kt):
                            n = exp_no(u, t, g, c)
                            act.wait_ge(s_score, n + 1)
                            src = score_ps[c % 2][:, :, :]
                            if len(heads) == 4:
                                src = src.rearrange("p a c -> p (a c)")[:, 0:4 * wd].rearrange("p (h c) -> p h c", h=4)
                            else:
                                src = src[:, :, 0:wd]
                            nc.scalar.activation(P[kt % 2][:, heads[0]:heads[-1] + 1, 0:wd], src, ACT.Exp).then_inc(s_exp, 1)
                            c += 1
                        flush()
                        if trailing and kt == 0:
                            pv_out(*trailing)
                        for name, tt in beside(u, g, kt, t, whole):
                            side_work(name, tt if name not in ("mt", "ot") else t, u, g)
                    trailing = (u, t, g)
                return trailing

            def silu(t, i):
                act.wait_ge(s_gu_ps, NHID * t + i + 1)
                if i >= 2:
                    act.wait_ge(s_hid, NHID * t + i - 1)
                nc.scalar.activation(P[i % 2][:, 0, :], score_ps[i % 2][:, 0, :], ACT.Silu).then_inc(s_silu, 1)

            def between(t, whole):
                f = whole != "first"
                pv_out(S, t, NG - 1)
                if f:
                    silu(t - 1, 0)
                    silu(t - 1, 1)
                for m in range(KC):
                    act.wait_ge(s_att_ps, KC * t + m + 1)
                    nc.scalar.copy(oT[:, m, :], side[:, :]).then_inc(s_att, 1)
                if f:
                    for i in range(2, 5):
                        silu(t - 1, i)
                high(QX, 0, t)
                high(QX, 1, t)
                if f:
                    silu(t - 1, 5)
                max_rows(X, t, 0)
                flush()

            for name in ("xt0", "xt1", "qs0", "ks0", "qs1", "ks1", "v0", "v1"):
                side_work(name, 0, S, 0)
            max_rows(S, 0, 0)
            flush()
            act.wait_ge(s_gw, 3)
            attention(S, 0, "first", None)
            between(0, "first")
            with act.Fori(0, LAST) as t:
                trailing = attention(X, t, "", None)
                attention(S, t + 1, "", trailing)
                between(t + 1, "")
            trailing = attention(X, LAST, "last", None)
            pv_out(*trailing)
            for m in range(KC):
                side_work(f"yt{m}", LAST, X, 0)
            for i in range(NHID):
                silu(LAST, i)

        @block.vector
        def _(dve):
            def norm(i, src, t):
                for c in range(NT):
                    nc.vector.bn_stats(stats[:, c, :], src[:, c, :]).then_inc(s_stat[i], 1)
                for c in range(NT):
                    wait_apart(dve, s_stat[i], NT * t + c + 1)
                    nc.vector.bn_aggr(mv[:, c, :], stats[:, c, :]).then_inc(s_aggr[i], 1)

            def norm_end(i, src, t):
                dve.wait_ge(s_rstd[i], t + 1)
                for c in range(NT):
                    nc.vector.tensor_scalar(ln[:, c, :], src[:, c, :], mv[:, c, 0:1], rstd[:, c:c + 1],
                                            ALU.subtract, ALU.mult).then_inc(s_ln[i], 1)

            def take_max(u, t, g, i):
                keys = 128 * (i % NT + 1) if u == S else T
                dve.wait_ge(s_max_ps, max_no(u, t, g, i) + 1)
                nc.vector.tensor_reduce(mx[g % 2][:, i % NT, i // NT:i // NT + 1], max_ps[i % 2][:, 0:keys], AX.X,
                                        ALU.max, negate=True).then_inc(s_max, 1)

            def left_over(w, m, t):
                n, b = split_no(w, m, t), SPLIT_PLACE[w, m] % 2
                dve.wait_ge(s_hi, n + 1)
                nc.vector.scalar_tensor_tensor(rest[b][:, :], side[:, :], SCALE if w in (QS, QX) else 1.0,
                                               parts[b][:, 0, :], ALU.mult, ALU.subtract).then_inc(s_rest, 1)

            def head_outputs(u, t, g):
                j = job(u, t, g)
                dve.wait_ge(s_ot_ps, j + 1)
                src = side[:, :].rearrange("p (c h e) -> p c h e", c=NT, h=GH)
                nc.vector.reciprocal(rden[g % 2][:, :, :], src[:, :, :, HD]).then_inc(s_rden, 1)
                dve.wait_ge(s_rden, j + 1)
                to = att[:, :, HD * GH * g:HD * GH * (g + 1)].rearrange("p c (h d) -> p c h d", d=HD)
                nc.vector.tensor_tensor(to, src[:, :, :, 0:HD], rden[g % 2][:, :, :].unsqueeze(3).broadcast_to([128, NT, GH, HD]),
                                        ALU.mult).then_inc(s_ot, 1)

            def attention(u, t, whole):
                for g in range(NG):
                    ahead = max_job(u, t, g, whole)
                    for kt in range(NT):
                        if ahead:
                            for i in range(4):
                                take_max(*ahead, 4 * kt + i)
                        for name, tt in beside(u, g, kt, t, whole):
                            if name == "ot":
                                head_outputs(*prev_job(u, t, g))
                            elif name[:2] in ("qs", "ks", "kx"):
                                left_over({"qs": QS, "ks": KS, "kx": KX}[name[:2]], int(name[2]), tt)
                        if whole != "last" and (u, g, kt) == (X, 0, 0):
                            norm_end(0, x_in, t + 1)
                        if whole != "first" and (u, g, kt) == (S, 0, 3):
                            dve.wait_ge(s_x2, t)
                            norm(2, x2, t - 1)
                        if whole != "first" and (u, g, kt) == (S, 1, 3):
                            norm_end(2, x2, t - 1)

            def hidden(t, i):
                dve.wait_ge(s_silu, NHID * t + i + 1)
                nc.vector.tensor_tensor(hid[:, i, :], score_ps[i % 2][:, 1, :], P[i % 2][:, 0, :], ALU.mult).then_inc(s_hid, 1)

            def output(t, half):
                dve.wait_ge(s_dn_ps, 2 * t + half + 1)
                if half == 0 and (not isinstance(t, int) or t > 0):
                    dve.wait_ge(s_out, 16 * t)
                nc.vector.tensor_tensor(y_out[:, 2 * half:2 * half + 2, :], score_ps[half][:, 0, :].rearrange("p (c d) -> p c d", c=2),
                                        x2[:, 2 * half:2 * half + 2, :], ALU.add).then_inc(s_y, 1)

            def between(t, whole):
                f = whole != "first"
                if f:
                    hidden(t - 1, 0)
                head_outputs(S, t, NG - 1)
                if f:
                    hidden(t - 1, 1)
                    hidden(t - 1, 2)
                for half in range(2):
                    dve.wait_ge(s_wo_ps, 2 * t + half + 1)
                    nc.vector.tensor_tensor(x1[:, 2 * half:2 * half + 2, :], side[:, :].rearrange("p (c d) -> p c d", c=2),
                                            x_in[:, 2 * half:2 * half + 2, :], ALU.add).then_inc(s_x1, 1)
                dve.wait_ge(s_x1, 2 * (t + 1))
                norm(1, x1, t)
                if f:
                    hidden(t - 1, 3)
                    hidden(t - 1, 4)
                norm_end(1, x1, t)
                left_over(QX, 0, t)
                left_over(QX, 1, t)
                if f:
                    hidden(t - 1, 5)
                for g in range(2):
                    for q in range(4):
                        for i in range(4):
                            take_max(X, t, g, 4 * q + i)
                        if f and (g, q) == (0, 1):
                            output(t - 1, 0)
                        if f and (g, q) == (1, 1):
                            output(t - 1, 1)

            def first_norm(t):
                dve.wait_ge(s_x, 16 * (t + 1))
                norm(0, x_in, t)

            first_norm(0)
            norm_end(0, x_in, 0)
            for w, m in ((QS, 0), (KS, 0), (QS, 1), (KS, 1)):
                left_over(w, m, 0)
            dve.wait_ge(s_wi, 16 * 3)
            for w_sb, w_i in ((Wg, wg_i), (Wu, wu_i), (Wd, wd_i)):
                nc.vector.tensor_scalar(w_sb[:, :, :].rearrange("p c n -> p (c n)"), w_i, 1.0 / 127.0, None,
                                        ALU.mult).then_inc(s_gw, 1)
            for g in range(2):
                for i in range(GH * NT):
                    take_max(S, 0, g, i)
            attention(S, 0, "first")
            between(0, "first")
            with dve.Fori(0, LAST) as t:
                first_norm(t + 1)
                attention(X, t, "")
                attention(S, t + 1, "")
                between(t + 1, "")
            attention(X, LAST, "last")
            head_outputs(X, LAST, NG - 1)
            dve.wait_ge(s_x2, B)
            norm(2, x2, LAST)
            norm_end(2, x2, LAST)
            for i in range(NHID):
                hidden(LAST, i)
            for half in range(2):
                output(LAST, half)



def kernel(**inputs):
    import numpy as np
    import ml_dtypes
    import concourse.bacc as bacc
    from concourse.bass_utils import run_bass_kernel_spmd as run

    bf = ml_dtypes.bfloat16
    a = {k: np.asarray(v) for k, v in inputs.items()}
    B, T, D = a["x"].shape
    NH = 16

    def three_parts(v):
        parts = []
        for _ in range(3):
            parts.append(v.astype(bf))
            v = v - parts[-1].astype(np.float64)
        return np.stack(parts)

    base = 2.0 ** (-8.0 / NH)
    slopes = np.array([base ** i for i in range(1, NH + 1)], np.float32).astype(np.float64)
    ramp = three_parts(slopes[:, None] * np.arange(T))
    ramp = np.stack([ramp, np.zeros_like(ramp)])
    fill = np.ones((3, NH, T), bf)
    at = np.arange(128)
    hidden = np.where(at[:, None] < at[None, :], -1e30, 0.0)
    masks = np.stack([hidden, hidden.T, np.eye(128)], 1).astype(bf)

    arrays = {
        "x": a["x"], "ctx": a["ctx_1024"],
        "wq": a["L0_attn_Wq"].T, "wk": a["L0_attn_Wk"].T, "wv": a["L0_attn_Wv"].T, "wo": a["L0_attn_Wo"].T,
        "w_gate": a["L0_ffn_w_gate"].T, "w_up": a["L0_ffn_w_up"].T, "w_down": a["L0_ffn_w_down"].T,
        "ramp": ramp, "fill": fill, "masks": masks,
    }
    arrays = {f"{k}_dram": np.ascontiguousarray(v) for k, v in arrays.items()}
    nc = bacc.Bacc("TRN2", target_bir_lowering=False, num_devices=1)
    ins = [nc.dram_tensor(k, v.shape, mybir.dt.from_np(v.dtype), kind="ExternalInput").ap() for k, v in arrays.items()]
    parts = nc.dram_tensor("parts_dram", (4, 3, D, T), mybir.dt.bfloat16, kind="Internal").ap()
    out = nc.dram_tensor("out_dram", (B, T, D), mybir.dt.float32, kind="ExternalOutput").ap()
    decoder_kernel(nc, *ins, parts, out)
    r = run(nc, [arrays], core_ids=[0])
    return r.results[0]["out_dram"]
```

```python
import concourse.bass as bass
from concourse import mybir
from contextlib import ExitStack


def decoder_kernel(nc, x, ctx, wq, wk, wv, wo, w_gate, w_up, w_down, ramp, fill, masks, parts_dram, out):
    f32, bf16, f32r, i32 = mybir.dt.float32, mybir.dt.bfloat16, mybir.dt.float32r, mybir.dt.int32
    ALU, ACT, AX = mybir.AluOpType, mybir.ActivationFunctionType, mybir.AxisListType

    B, T, D = x.shape
    HD = 16
    NH = D // HD
    HID = w_gate.shape[1]
    NT = T // 128
    KC = D // 128
    NHID = HID // 128
    NG = 4
    GH = NH // NG
    HH = NH // 2
    QP = [0, 0, 1, 1, 0, 2]
    KP = [0, 1, 0, 1, 2, 0]
    R_MAX = 16 * len(QP) + 3
    R_ALL = R_MAX + 3
    S, X = 0, 1
    QS, KS, KX, QX = 0, 1, 2, 3
    SCALE = HD ** -0.5
    EPS = 1e-5
    W_SCALE = 1.0 / 127.0
    LAST = B - 1

    def width(u, kt):
        return T - 128 * kt if u == S else T

    def chunks(u, kt):
        n = max(1, 512 // width(u, kt))
        return [list(range(i, i + n)) for i in range(0, GH, n)]

    def halves(u, kt):
        cs = list(enumerate(chunks(u, kt), sum(len(chunks(u, k)) for k in range(kt))))
        return cs[:(len(cs) + 1) // 2], cs[(len(cs) + 1) // 2:]

    EXPS = [sum(len(chunks(u, kt)) for kt in range(NT)) for u in (S, X)]
    RING = 3

    def score_bank(u, g, c):
        return (NG * EXPS[S] * u + EXPS[u] * g + c) % RING

    def max_bank(i):
        return i % 2

    def is_at(t, value):
        return isinstance(t, int) and t == value

    def self_before(u, t):
        return t if u == S else B if is_at(t, LAST) else t + 2

    def cross_before(u, t):
        return t if u == X else 0 if is_at(t, 0) else t - 1

    def job(u, t, g):
        return NG * (self_before(u, t) + cross_before(u, t)) + g

    def exp_no(u, t, g, c):
        return NG * EXPS[S] * self_before(u, t) + NG * EXPS[X] * cross_before(u, t) + EXPS[u] * g + c

    def max_no(u, t, g, i):
        return GH * NT * job(u, t, g) + i

    SPLIT_PLACE = {(QS, 0): 0, (KS, 0): 1, (QS, 1): 2, (KS, 1): 3, (KX, 0): 4, (QX, 0): 5, (QX, 1): 6, (KX, 1): 7}

    def split_no(w, m, t):
        place = SPLIT_PLACE[w, m]
        if w in (QS, KS):
            return place if is_at(t, 0) else 8 * t - 4 + place
        return 8 * t + place if is_at(t, LAST) else 8 * t + 4 + place

    BESIDE = {
        (X, 0): [("", ""), ("mt", "ot"), ("", "xt0"), ("xt1", "qs0")],
        (X, 1): [("ks0", "at0"), ("mt at1", "ot"), ("wo0", "wo1"), ("v0", "v1")],
        (X, 2): [("qs1", "ks1"), ("mt", "ot"), ("kx0", ""), ("", "qx0")],
        (X, 3): [("qx1", ""), ("mt", "ot"), ("kx1", ""), ("", "")],
        (S, 0): [("", ""), ("mt", "ot"), ("", ""), ("", "")],
        (S, 1): [("", "yt0"), ("mt yt1", "ot"), ("gu0", "gu1"), ("gu2", "gu3")],
        (S, 2): [("gu4", "gu5"), ("mt", "ot"), ("dn0", "dn1"), ("gu6", "gu7")],
        (S, 3): [("gu8", "gu9"), ("mt", "ot"), ("gu10", "gu11"), ("", "dn2 dn3")],
    }
    PLACES = [(u, g, kt, end) for u in (X, S) for g in range(NG) for kt in range(NT) for end in range(2)]
    ALL = [(u, g, name) for u, g, kt, end in PLACES for name in BESIDE[u, g][kt][end].split()]

    def side_bank(u, g, name):
        if name[:2] in ("mt", "ot"):
            return ALL.index((u, g, name)) % 2
        return [n for _, _, n in ALL].index(name) % 2

    def kind_no(name):
        kind = name.rstrip("0123456789")
        return kind, int(name[len(kind):] or 0)

    def sequence(u, name, t):
        kind, _ = kind_no(name)
        return {"xt": t + 2, "qs": t + 2, "ks": t + 2, "v": t + 2, "at": t + 1, "wo": t + 1, "kx": t + 1, "qx": t + 1,
                "yt": t - 2, "gu": t - 2, "dn": t - 2}.get(kind, t)

    def present(u, t, g, name):
        kind, _ = kind_no(name)
        if not isinstance(t, int):
            return True
        if u == S and t in (0, 1):
            return kind == "mt" and (g < NG - 1 or t == 1) or kind == "ot" and g > 0
        if u == X and t == LAST - 1:
            return kind not in ("xt", "qs", "ks", "v") and not (kind == "mt" and g == NG - 1)
        if u == X and t == LAST:
            return kind == "mt" and g < NG - 1 or kind == "ot" and g > 0
        return True

    def beside(u, t, g, kt, end, back=0):
        n = PLACES.index((u, g, kt, end)) - back
        if n < 0 or PLACES[n][0] != u:
            return []
        _, g, kt, end = PLACES[n]
        return [(name, g) for name in BESIDE[u, g][kt][end].split() if present(u, t, g, name)]

    LINK = ["xt0", "xt1", "at0", "at1", "qs0", "ks0", "wo0", "wo1", "v0", "v1", "qs1", "ks1", "kx0", "qx0", "qx1", "kx1"]
    FIRST = ["xt0", "xt1", "qs0", "ks0", "qs1", "ks1", "v0", "v1"]
    FFN = ["yt0", "yt1"] + [f"gu{i}" for i in range(NHID)] + ["dn0", "dn1"] + [
        f"gu{i}" for i in range(NHID, 2 * NHID)] + ["dn2", "dn3"]

    def next_job(u, t, g):
        if g < NG - 1:
            return u, t, g + 1
        if u == S:
            return (S, 1, 0) if is_at(t, 0) else (X, t - 1, 0)
        return (X, LAST, 0) if is_at(t, LAST - 1) else (S, t + 2, 0)

    def prev_job(u, t, g):
        if g:
            return u, t, g - 1
        if u == S:
            return (S, 0, NG - 1) if is_at(t, 1) else (X, t - 2, NG - 1)
        return (X, LAST - 1, NG - 1) if is_at(t, LAST) else (S, t + 1, NG - 1)

    def max_job(u, t, g):
        if g < 2:
            return u, t, g + 2
        if u == S:
            return None if is_at(t, 0) else (X, t - 1, g - 2)
        return None if isinstance(t, int) and t >= LAST - 1 else (S, t + 2, g - 2)

    es = ExitStack()
    with es:
        def sb(name, shape, dt=f32):
            return es.enter_context(nc.sbuf_tensor(name, shape, dt))

        def sem(name):
            return es.enter_context(nc.semaphore(name))

        LQ = [sb("lq_self", [128, NH, T], bf16), sb("lq_cross", [128, NH, T], bf16)]
        LK = [sb("lk_self", [128, NH, T], bf16), sb("lk_cross", [128, NH, T], bf16)]
        V = [sb("v_self", [128, NT, NH, 2 * HD]), sb("v_cross", [128, NT, NH, 2 * HD])]
        P = [sb(f"probs{i}", [128, GH, T]) for i in range(2)]
        x_in = sb("x_in", [128, NT, D])
        ctx_in = sb("ctx_in", [128, NT, D])
        x1 = sb("x1", [128, NT, D])
        x2 = sb("x2", [128, NT, D])
        att = sb("att", [128, NT, D])
        ln = sb("ln", [128, NT, D])
        aT = [sb(f"aT_{n}", [128, KC, T], f32r) for n in ("hi", "lo")]
        hid = [sb(f"hid_{n}", [128, NHID, T // 2], f32r) for n in ("hi", "lo")]
        flat = ln[:, :, :].rearrange("p c d -> p (c d)")
        oT = flat.rearrange("p (c t) -> p c t", c=KC)
        hid32, gate = ([flat[:, T // 2 * (2 * j + i):T // 2 * (2 * j + i + 1)] for i in range(2)] for j in range(2))
        parts = [sb(f"parts{i}", [128, 3, T], bf16) for i in range(2)]
        rest = [sb(f"rest{i}", [128, T]) for i in range(2)]
        pv_sb = sb("pv_sb", [128, T])
        mx = [sb(f"mx{i}", [128, NT, GH]) for i in range(2)]
        mxr = [sb(f"mxr{i}", [128, 2, NT, GH]) for i in range(2)]
        mxp = [sb(f"mxp{i}", [128, NT, 3, GH], bf16) for i in range(2)]
        mT = [sb(f"mT{i}", [3 * GH, T], bf16) for i in range(2)]
        rden = [sb(f"rden{i}", [128, NT, GH]) for i in range(2)]
        stats = sb("stats", [128, NT, 6])
        mv = sb("mv", [128, NT, 2])
        var_eps = sb("var_eps", [128, NT])
        rstd = sb("rstd", [128, NT])
        mhalf = sb("mhalf", [128, NT])
        ident = sb("ident", [128, 128])
        identb = sb("identb", [128, 128], bf16)
        maskb = sb("maskb", [128, 2, 128], bf16)
        Wo = sb("wo_sb", [128, KC, D])
        Wq, Wk, Wv = ([sb(f"w{n}_{a}", [128, KC, D], f32r) for a in ("hi", "lo")] for n in "qkv")
        Wg, Wu = ([sb(f"w{n}_{a}", [128, KC, HID], f32r) for a in ("hi", "lo")] for n in "gu")
        Wd = [sb(f"wd_{a}", [128, NHID, D], f32r) for a in ("hi", "lo")]
        wq_in, wk_in, wv_in = att[:, 0:KC, :], att[:, KC:2 * KC, :], x2[:, 0:KC, :]
        wg_in = P[0][:, :, :].rearrange("p h t -> p (h t)").bitcast(i32)[:, 0:KC * HID].rearrange("p (c n) -> p c n", c=KC)
        wu_in = P[1][:, :, :].rearrange("p h t -> p (h t)").bitcast(i32)[:, 0:KC * HID].rearrange("p (c n) -> p c n", c=KC)
        wd_in = [x1[:, :, :].bitcast(i32), x2[:, NT - (NHID - NT):NT, :].bitcast(i32)]

        score_ps = [es.enter_context(nc.psum_tensor(f"score_ps{i}", [128, 512], f32)) for i in range(RING)]
        max_ps = [es.enter_context(nc.psum_tensor(f"max_ps{i}", [128, 512], f32)) for i in range(2)]
        pv_ps = es.enter_context(nc.psum_tensor("pv_ps", [128, 512], f32))
        side_ps = [es.enter_context(nc.psum_tensor(f"side{i}", [128, 512], f32)) for i in range(2)]

        s_const, s_w, s_wi, s_x, s_ctx, s_out = (sem(n) for n in ("const_in", "w_in", "wi_in", "x_in", "ctx_in", "out"))
        s_parts_out = sem("parts_out")
        s_rows = [[sem(f"rows_{u}{m}") for m in range(2)] for u in "sx"]
        s_mrow = [sem(f"mrow{i}") for i in range(2)]
        s_carry = sem("carries_waits")
        s_set, s_ident, s_whi, s_w_set = sem("set"), sem("identity"), sem("w_hi"), sem("w_set")
        s_max_ps, s_max = sem("max_ps"), sem("max_taken")
        s_mpart, s_mt_ps, s_mt = sem("max_parts"), sem("mt_ps"), sem("mt_taken")
        s_score, s_exp, s_pv, s_pvout = sem("score_ps"), sem("exp"), sem("pv_ps"), sem("pv_taken")
        s_ot_ps, s_rden, s_ot = sem("ot_ps"), sem("rden"), sem("ot_taken")
        s_sp_ps, s_hi, s_rest, s_mid, s_lo = (sem(n) for n in ("split_ps", "part_hi", "part_rest", "part_mid", "part_lo"))
        s_stat, s_aggr, s_vare, s_rstd, s_ln = ([sem(f"{n}{i}") for i in range(3)]
                                               for n in ("ln_stat", "ln_aggr", "ln_vare", "ln_rstd", "ln_done"))
        s_xt_ps, s_xhi, s_xt, s_yt_ps, s_yhi, s_yt = (sem(n) for n in ("xt_ps", "xt_hi", "xt_taken", "yt_ps", "yt_hi", "yt_taken"))
        s_v_ps, s_v, s_vx = sem("v_ps"), sem("v_taken"), sem("v_cross")
        s_att_ps, s_att, s_wo_ps, s_x1, s_x2 = (sem(n) for n in ("attT_ps", "attT_taken", "wo_ps", "x1", "x2"))
        s_again, s_moved = sem("x_again"), sem("x1_moved")
        s_gu_ps, s_tanh, s_gate, s_hid, s_hhi, s_hlo, s_dn_ps, s_y = (
            sem(n) for n in ("gate_up_ps", "tanh", "gate", "hidden", "hidden_hi", "hidden_lo", "down_ps", "y"))

        block = es.enter_context(nc.Block())

        def wait_apart(engine, semaphore, value):
            engine.wait_ge(semaphore, value)
            engine.sem_inc(s_carry, 1)

        @block.sync
        def _(sp):
            def load_x(t):
                if not is_at(t, 0):
                    wait_apart(sp, s_ln[0], NT * t)
                sp.dma_start(x_in[:, :, :], x[t, :, :].rearrange("(c p) d -> p c d", p=128)).then_inc(s_x, 16)

            def load_x_again(t):
                if is_at(t, 0):
                    wait_apart(sp, s_w_set, 7)
                else:
                    wait_apart(sp, s_moved, t)
                    wait_apart(sp, s_ln[1], NT * t)
                sp.dma_start(x1[:, :, :], x[t, :, :].rearrange("(c p) d -> p c d", p=128)).then_inc(s_again, 16)

            def load_ctx(t):
                if not is_at(t, 0):
                    wait_apart(sp, s_sp_ps, split_no(KX, 1, t - 1) + 1)
                    wait_apart(sp, s_vx, t)
                sp.dma_start(ctx_in[:, :, :], ctx[t, :, :].rearrange("(c p) d -> p c d", p=128)).then_inc(s_ctx, 16)

            def split(w, m, t):
                n = split_no(w, m, t)
                sp.wait_ge(s_lo, n + 1)
                sp.dma_start(parts_dram[w, :, 128 * m:128 * m + 128, :].rearrange("a p c -> p a c"),
                             parts[SPLIT_PLACE[w, m] % 2][:, :, :]).then_inc(s_parts_out, 16)
                wait_apart(sp, s_parts_out, 16 * n + 16)
                if w in (QX, KX) and m == 1 and not is_at(t, 0):
                    wait_apart(sp, s_score, exp_no(X, t - 1, NG - 1, EXPS[X] - 1) + 1)
                u = S if w in (QS, KS) else X
                rows, order = (LQ[u], QP) if w in (QS, QX) else (LK[u], KP)
                for b, part in enumerate(order):
                    sp.dma_start(rows[16 * b:16 * b + 16, HH * m:HH * m + HH, :],
                                 parts_dram[w, part, 128 * m:128 * m + 128, :].rearrange("(h d) c -> d h c", d=HD)
                                 ).then_inc(s_rows[u][m], 16)

            def store(t):
                sp.wait_ge(s_y, NT * (t + 2))
                sp.dma_start(out[t, :, :].rearrange("(c p) d -> p c d", p=128), x2[:, :, :]).then_inc(s_out, 16)

            load_x(0)
            for to, w in ((wq_in, wq), (wk_in, wk), (wv_in, wv), (Wo[:, :, :], wo)):
                sp.dma_start(to, w.rearrange("(c p) n -> p c n", p=128)).then_inc(s_w, 16)
            sp.dma_start(maskb[:, :, :], masks[:, 0:2, :]).then_inc(s_const, 16)
            sp.dma_start(identb[:, :], masks[:, 2, :]).then_inc(s_const, 16)
            for u in (S, X):
                sp.dma_start(LQ[u][R_MAX - 3:R_MAX, :, :], fill).then_inc(s_const, 16)
                sp.dma_start(LK[u][R_MAX:R_ALL, :, :], fill).then_inc(s_const, 16)
                sp.dma_start(LK[u][R_MAX - 3:R_MAX, :, :], ramp[u, :, :, :]).then_inc(s_const, 16)
            load_ctx(0)
            sp.dma_start(wg_in, w_gate.rearrange("(c p) n -> p c n", p=128)).then_inc(s_wi, 16)
            sp.dma_start(wu_in, w_up.rearrange("(c p) n -> p c n", p=128)).then_inc(s_wi, 16)
            sp.dma_start(wd_in[0], w_down[0:128 * NT, :].rearrange("(c p) n -> p c n", p=128)).then_inc(s_wi, 16)
            sp.dma_start(wd_in[1], w_down[128 * NT:HID, :].rearrange("(c p) n -> p c n", p=128)).then_inc(s_wi, 16)
            SELF, CROSS = ((QS, 0), (KS, 0), (QS, 1), (KS, 1)), ((KX, 0), (QX, 0), (QX, 1), (KX, 1))
            for w, m in SELF:
                split(w, m, 0)
            load_x(1)
            load_x_again(0)
            for w, m in SELF:
                split(w, m, 1)
            for w, m in CROSS:
                split(w, m, 0)
            load_ctx(1)

            with sp.Fori(0, LAST - 1) as t:
                load_x(t + 2)
                load_x_again(t + 1)
                for w, m in SELF:
                    split(w, m, t + 2)
                for w, m in CROSS:
                    split(w, m, t + 1)
                load_ctx(t + 2)
                store(t)
            load_x_again(LAST)
            for w, m in CROSS:
                split(w, m, LAST)
            store(LAST - 1)
            store(LAST)
            sp.wait_ge(s_out, 16 * (B + 1))

        @block.gpsimd
        def _(pool):
            nc.gpsimd.memset(ident[:, :], 0.0).then_inc(s_ident, 1)
            nc.gpsimd.memset(mhalf[:, :], -0.5).then_inc(s_set, 1)
            for u in (S, X):
                nc.gpsimd.memset(V[u][:, :, :, HD:2 * HD], 1.0).then_inc(s_set, 1)
            pool.wait_ge(s_ident, 1)
            nc.gpsimd.affine_select(out=ident[:, :], in_=ident[:, :], compare_op=ALU.not_equal, fill=1.0, base=0,
                                    pattern=[[-1, 128]], channel_multiplier=1).then_inc(s_ident, 1)

            def norm(i, t):
                wait_apart(pool, s_aggr[i], NT * (t + 1))
                nc.gpsimd.tensor_scalar(var_eps[:, :], mv[:, :, 1], EPS, None, ALU.add).then_inc(s_vare[i], 1)
                pool.wait_ge(s_vare[i], t + 1)
                nc.gpsimd.tensor_tensor(rstd[:, :], var_eps[:, :], mhalf[:, :], ALU.pow).then_inc(s_rstd[i], 1)

            def max_parts(u, t, g):
                j, b = job(u, t, g), g % 2
                left = mxr[b]
                wait_apart(pool, s_max, max_no(u, t, g, GH * NT - 1) + 1)
                nc.gpsimd.tensor_copy(mxp[b][:, :, 0, :], mx[b][:, :, :]).then_inc(s_mpart, 1)
                pool.wait_ge(s_mpart, 5 * j + 1)
                nc.gpsimd.tensor_tensor(left[:, 0, :, :], mx[b][:, :, :], mxp[b][:, :, 0, :], ALU.subtract).then_inc(s_mpart, 1)
                wait_apart(pool, s_mpart, 5 * j + 2)
                nc.gpsimd.tensor_copy(mxp[b][:, :, 1, :], left[:, 0, :, :]).then_inc(s_mpart, 1)
                pool.wait_ge(s_mpart, 5 * j + 3)
                nc.gpsimd.tensor_tensor(left[:, 1, :, :], left[:, 0, :, :], mxp[b][:, :, 1, :], ALU.subtract).then_inc(s_mpart, 1)
                wait_apart(pool, s_mpart, 5 * j + 4)
                nc.gpsimd.tensor_copy(mxp[b][:, :, 2, :], left[:, 1, :, :]).then_inc(s_mpart, 1)

            def split(w, m, t):
                n, b = split_no(w, m, t), SPLIT_PLACE[w, m] % 2
                wait_apart(pool, s_rest, n + 1)
                nc.gpsimd.tensor_copy(parts[b][:, 1, :], rest[b][:, :]).then_inc(s_mid, 1)
                pool.wait_ge(s_mid, n + 1)
                nc.gpsimd.tensor_tensor(parts[b][:, 2, :], rest[b][:, :], parts[b][:, 1, :], ALU.subtract).then_inc(s_lo, 1)

            def v_cross(t):
                if not is_at(t, 0):
                    pool.wait_ge(s_pv, NT * job(X, t - 1, NG))
                wait_apart(pool, s_ctx, 16 * (t + 1))
                nc.gpsimd.tensor_copy(V[X][:, :, :, 0:HD],
                                      ctx_in[:, :, :].rearrange("p c (h d) -> p c h d", d=HD)).then_inc(s_vx, 1)

            def move_x1(t):
                wait_apart(pool, s_x1, 2 * (t + 1))
                wait_apart(pool, s_out, 16 * (t + 1))
                nc.gpsimd.tensor_copy(x2[:, :, :], x1[:, :, :]).then_inc(s_moved, 1)

            def hidden_low(t, k):
                pool.wait_ge(s_hhi, 2 * NHID * t + k + 1)
                nc.gpsimd.tensor_tensor(hid[1][:, k % NHID, :], hid32[k % 2], hid[0][:, k % NHID, :].bitcast(f32),
                                        ALU.subtract).then_inc(s_hlo, 1)

            def side_work(name, t):
                kind, m = kind_no(name)
                if kind in ("qs", "ks", "kx", "qx"):
                    split({"qs": QS, "ks": KS, "kx": KX, "qx": QX}[kind], m, t)
                elif kind == "gu":
                    hidden_low(t, m)

            def attention(u, t):
                for g in range(NG):
                    for kt in range(NT):
                        for end in range(2):
                            for name, _ in beside(u, t, g, kt, end):
                                side_work(name, sequence(u, name, t))
                        if (u, g, kt) == (X, 0, 0) and not (isinstance(t, int) and t >= LAST - 1):
                            norm(0, t + 2)
                        if (u, g, kt) == (X, 0, 0):
                            move_x1(t)
                        if (u, g, kt) == (X, 1, 3) and not is_at(t, LAST):
                            norm(1, t + 1)
                        if (u, g, kt) == (S, 0, 3) and not (isinstance(t, int) and t <= 1):
                            norm(2, t - 2)
                            v_cross(t - 1)
                        if (u, g, kt) == (S, 0, 2) and is_at(t, 0):
                            v_cross(0)
                        if (u, g, kt) == (S, 2, 0) and is_at(t, 0):
                            norm(0, 1)
                    ahead = max_job(u, t, g)
                    if ahead:
                        max_parts(*ahead)

            pool.sem_inc(s_hlo, 2 * NHID)
            pool.wait_ge(s_set, 1)
            norm(0, 0)
            for w, m in ((QS, 0), (KS, 0), (QS, 1), (KS, 1)):
                split(w, m, 0)
            max_parts(S, 0, 0)
            max_parts(S, 0, 1)
            attention(S, 0)
            for name in LINK:
                side_work(name, sequence(X, name, -1))
                if name == "wo1":
                    norm(1, 0)
            max_parts(S, 1, 0)
            max_parts(S, 1, 1)
            attention(S, 1)
            with pool.Fori(0, LAST - 1) as t:
                attention(X, t)
                attention(S, t + 2)
            attention(X, LAST - 1)
            v_cross(LAST)
            norm(2, LAST - 1)
            max_parts(X, LAST, 0)
            for name in FFN:
                side_work(name, LAST - 1)
            max_parts(X, LAST, 1)
            attention(X, LAST)
            norm(2, LAST)
            for name in FFN:
                side_work(name, LAST)

        @block.tensor
        def _(pe):
            class Bank:
                def __init__(self):
                    self.free = None

                def take(self, free):
                    if self.free:
                        pe.wait_ge(*self.free)
                    self.free = free

            pv_bank = Bank()
            score_banks, max_banks, side_banks = ([Bank() for _ in range(n)] for n in (RING, 2, 2))

            def transpose4(src, m, at, sem_to, free):
                ps = side_ps[at]
                side_banks[at].take(free)
                for c in range(NT):
                    last = nc.tensor.transpose(ps[:, 128 * c:128 * c + 128], src[:, c, 128 * m:128 * m + 128], ident[:, :])
                last.then_inc(sem_to, 1)

            def three_passes(to, a, b, where_a, where_b, k, n):
                for i, (x, y) in enumerate(((0, 0), (0, 1), (1, 0))):
                    last = nc.tensor.matmul(to, a[x][where_a], b[y][where_b], start=k == i == 0, stop=k == n - 1 and i == 2)
                return last

            def project(w_sb, m, t, at, sem_to, free):
                side_banks[at].take(free)
                pe.wait_ge(s_xt, KC * (t + 1))
                for k in range(KC):
                    last = three_passes(side_ps[at][:, :], w_sb, aT, (slice(None), k, slice(128 * m, 128 * m + 128)),
                                        (slice(None), k, slice(None)), k, KC)
                last.then_inc(sem_to, 1)

            def values(half, t, at):
                side_banks[at].take((s_v, 2 * t + half + 1))
                for c in range(2):
                    r = 2 * half + c
                    for k in range(KC):
                        last = three_passes(side_ps[at][:, 256 * c:256 * c + 256], aT, Wv,
                                            (slice(None), k, slice(128 * r, 128 * r + 128)), (slice(None), k, slice(None)), k, KC)
                last.then_inc(s_v_ps, 1)

            def out_projection(half, t, at):
                ps = side_ps[at]
                side_banks[at].take((s_x1, 2 * t + half + 1))
                pe.wait_ge(s_att, KC * (t + 1))
                for c in range(2):
                    r = 2 * half + c
                    for k in range(KC):
                        last = nc.tensor.matmul(ps[:, 256 * c:256 * c + 256], oT[:, k, 128 * r:128 * r + 128],
                                                Wo[:, k, :], start=k == 0, stop=k == KC - 1)
                last.then_inc(s_wo_ps, 1)

            def max_transposes(u, t, g, at):
                j = job(u, t, g)
                side_banks[at].take((s_mt, j + 1))
                pe.wait_ge(s_mpart, 5 * j + 5)
                for c in range(NT):
                    last = nc.tensor.transpose(side_ps[at][:, :].bitcast(bf16)[0:3 * GH, 128 * c:128 * c + 128],
                                               mxp[g % 2][:, c, :, :].rearrange("p a h -> p (a h)"), identb[:, :])
                last.then_inc(s_mt_ps, 1)

            def out_transposes(u, t, g, at):
                j = job(u, t, g)
                side_banks[at].take((s_ot, j + 1))
                pe.wait_ge(s_pvout, j + 1)
                for c in range(NT):
                    last = nc.tensor.transpose(side_ps[at][:, 128 * c:128 * c + 128], pv_sb[:, 128 * c:128 * c + 128], ident[:, :])
                last.then_inc(s_ot_ps, 1)

            def gate_up(t, k, at):
                half, i = k // NHID, k % NHID
                side_banks[at].take((s_hid, 2 * NHID * t + k + 1))
                pe.wait_ge(s_yt, KC * (t + 1))
                for j, w_sb in enumerate((Wg, Wu)):
                    for k in range(KC):
                        last = three_passes(side_ps[at][:, 256 * j:256 * j + 256], w_sb, aT,
                                            (slice(None), k, slice(128 * i, 128 * i + 128)),
                                            (slice(None), k, slice(256 * half, 256 * half + 256)), k, KC)
                last.then_inc(s_gu_ps, 1)

            def down(t, r, at):
                side_banks[at].take((s_y, NT * (t + 1) + r + 1))
                pe.wait_ge(s_hlo, NHID * (2 * t + 2 + r // 2 + 1))
                for k in range(NHID):
                    last = three_passes(side_ps[at][:, 0:256], hid, Wd, (slice(None), k, slice(128 * (r % 2), 128 * (r % 2) + 128)),
                                        (slice(None), k, slice(None)), k, NHID)
                last.then_inc(s_dn_ps, 1)

            def side_work(u, t, g, name, tt):
                (kind, m), at = kind_no(name), side_bank(u, g, name)
                if kind == "mt":
                    max_transposes(*next_job(u, t, g), at)
                elif kind == "ot":
                    out_transposes(*prev_job(u, t, g), at)
                elif kind == "xt":
                    pe.wait_ge(s_ln[0], NT * (tt + 1))
                    transpose4(ln, m, at, s_xt_ps, (s_xt, KC * tt + m + 1))
                elif kind == "yt":
                    pe.wait_ge(s_ln[2], NT * (tt + 1))
                    transpose4(ln, m, at, s_yt_ps, (s_yt, KC * tt + m + 1))
                elif kind in ("qs", "ks"):
                    w = QS if kind == "qs" else KS
                    project(Wq if w == QS else Wk, m, tt, at, s_sp_ps, (s_rest, split_no(w, m, tt) + 1))
                elif kind == "kx":
                    pe.wait_ge(s_ctx, 16 * (tt + 1))
                    transpose4(ctx_in, m, at, s_sp_ps, (s_rest, split_no(KX, m, tt) + 1))
                elif kind == "qx":
                    pe.wait_ge(s_ln[1], NT * (tt + 1))
                    transpose4(ln, m, at, s_sp_ps, (s_rest, split_no(QX, m, tt) + 1))
                elif kind == "at":
                    pe.wait_ge(s_ot, job(S, tt, NG - 1) + 1)
                    transpose4(att, m, at, s_att_ps, (s_att, KC * tt + m + 1))
                elif kind == "wo":
                    out_projection(m, tt, at)
                elif kind == "v":
                    values(m, tt, at)
                elif kind == "gu":
                    gate_up(tt, m, at)
                else:
                    down(tt, m, at)

            def max_product(u, t, g, i):
                n, b = max_no(u, t, g, i), max_bank(i)
                h, r = GH * g + i // NT, i % NT
                if i == 0 and g % 2 == 0:
                    pe.wait_ge(s_rows[u][g // 2], 16 * 12 * (t + 1))
                max_banks[b].take((s_max, n + 1))
                keys = 128 * (r + 1) if u == S else T
                last = nc.tensor.matmul(max_ps[b][:, 0:keys], LQ[u][0:R_MAX, h, 128 * r:128 * r + 128],
                                        LK[u][0:R_MAX, h, 0:keys], start=True, stop=u == X)
                if u == S:
                    last = nc.tensor.matmul(max_ps[b][:, keys - 128:keys], identb[:, :], maskb[:, 0, :],
                                            start=False, stop=True)
                last.then_inc(s_max_ps, 1)

            def scores(u, t, g, kt, c, heads):
                b, wd = score_bank(u, g, c), width(u, kt)
                score_banks[b].take((s_exp, exp_no(u, t, g, c) + 1))
                for i, hh in enumerate(heads):
                    h = GH * g + hh
                    last = nc.tensor.matmul(score_ps[b][:, wd * i:wd * i + wd], LK[u][0:R_ALL, h, 128 * kt:128 * kt + 128],
                                            LQ[u][0:R_ALL, h, T - wd:T], start=True, stop=u == X)
                    if u == S:
                        last = nc.tensor.matmul(score_ps[b][:, wd * i:wd * i + 128], identb[:, :], maskb[:, 1, :],
                                                start=False, stop=True)
                last.then_inc(s_score, 1)

            def weigh(u, t, g, kt):
                if kt == 0:
                    pv_bank.take((s_pvout, job(u, t, g) + 1))
                pe.wait_ge(s_exp, exp_no(u, t, g, sum(len(chunks(u, k)) for k in range(kt + 1)) - 1) + 1)
                wd = width(u, kt)
                for hh in range(GH):
                    last = nc.tensor.matmul(pv_ps[32 * hh:32 * hh + 32, T - wd:T], V[u][:, kt, GH * g + hh, :],
                                            P[kt % 2][:, hh, 0:wd], start=kt == 0, stop=kt == NT - 1)
                last.then_inc(s_pv, 1)

            def attention(u, t, trailing):
                for g in range(NG):
                    pe.wait_ge(s_mrow[g % 2], 48 * (NG // 2 * (self_before(u, t) + cross_before(u, t)) + g // 2 + 1))
                    ahead = max_job(u, t, g)
                    for kt in range(NT):
                        if u == S and g == 0 and kt == 0:
                            pe.wait_ge(s_v, 2 * (t + 1))
                        if u == X and g == 0 and kt == 0:
                            pe.wait_ge(s_vx, t + 1)
                        for end, cs in enumerate(halves(u, kt)):
                            for i, (c, heads) in enumerate(cs):
                                if ahead and i == 0:
                                    max_product(*ahead, 4 * kt + 2 * end)
                                scores(u, t, g, kt, c, heads)
                            if ahead and not cs:
                                max_product(*ahead, 4 * kt + 2 * end)
                            if end:
                                if ahead:
                                    max_product(*ahead, 4 * kt + 3)
                                if trailing:
                                    weigh(*trailing)
                            for name, _ in beside(u, t, g, kt, end):
                                side_work(u, t, g, name, sequence(u, name, t))
                            if ahead and not end:
                                max_product(*ahead, 4 * kt + 1)
                        trailing = (u, t, g, kt)
                return trailing

            def loop_entry(t):
                for bank in side_banks:
                    bank.free = (s_y, NT * (t + 1))
                for i in range(2):
                    max_banks[i].free = (s_max, max_no(X, t, 1, GH * NT - 2 + i) + 1)
                pv_bank.free = (s_pvout, job(X, t, 0))
                for c in range(EXPS[S] - RING, EXPS[S]):
                    score_banks[score_bank(S, NG - 1, c)].free = (s_exp, exp_no(S, t + 1, NG - 1, c) + 1)

            pe.wait_ge(s_ident, 2)
            pe.wait_ge(s_const, 16 * 8)
            pe.wait_ge(s_w, 16 * 4)
            pe.wait_ge(s_w_set, 3)
            pe.wait_ge(s_set, 3)
            for name in FIRST:
                side_work(X, -2, 0, name, 0)
            for g in range(2):
                for i in range(GH * NT):
                    max_product(S, 0, g, i)
                if g == 0:
                    max_transposes(S, 0, 0, 0)
            trailing = attention(S, 0, None)
            weigh(*trailing)
            out_transposes(S, 0, NG - 1, 0)
            for name in LINK:
                side_work(X, -1, 0, name, sequence(X, name, -1))
            for g in range(2):
                for i in range(GH * NT):
                    max_product(S, 1, g, i)
                if g == 0:
                    max_transposes(S, 1, 0, 0)
            trailing = attention(S, 1, None)
            pe.wait_ge(s_ot, job(S, 1, NG - 2) + 1)
            pe.wait_ge(s_mt, job(X, 0, 0) + 1)
            pe.wait_ge(s_w_set, 7)
            with pe.Fori(0, LAST - 1) as t:
                loop_entry(t)
                trailing = attention(X, t, (S, t + 1, NG - 1, NT - 1))
                trailing = attention(S, t + 2, trailing)
            loop_entry(LAST - 1)
            trailing = attention(X, LAST - 1, (S, LAST, NG - 1, NT - 1))
            weigh(*trailing)
            out_transposes(X, LAST - 1, NG - 1, 0)
            for i in range(GH * NT):
                max_product(X, LAST, 0, i)
            for n, name in enumerate(FFN):
                side_work(S, LAST + 1, 0, name, LAST - 1)
                if n == 1:
                    max_transposes(X, LAST, 0, 1)
                if n < GH * NT:
                    max_product(X, LAST, 1, n)
            trailing = attention(X, LAST, None)
            weigh(*trailing)
            out_transposes(X, LAST, NG - 1, 0)
            for name in FFN:
                side_work(S, LAST + 2, 0, name, LAST)

        @block.scalar
        def _(act):
            def max_rows(u, t, g, at):
                act.wait_ge(s_mt_ps, job(u, t, g) + 1)
                nc.scalar.copy(mT[g % 2][:, :], side_ps[at][:, :].bitcast(bf16)[0:3 * GH, 0:T]).then_inc(s_mt, 1)

            def max_rows_load(u, t, g):
                act.wait_ge(s_mt, job(u, t, g) + 1)
                for a in range(3):
                    act.dma_start(LQ[u][R_MAX + a:R_MAX + a + 1, GH * g:GH * g + GH, :],
                                  mT[g % 2][GH * a:GH * a + GH, :]).then_inc(s_mrow[g % 2], 16)

            def pv_out(u, t, g):
                j = job(u, t, g)
                act.wait_ge(s_pv, NT * (j + 1))
                nc.scalar.copy(pv_sb[:, :], pv_ps[:, :]).then_inc(s_pvout, 1)

            def high(w, m, t, at):
                n, b = split_no(w, m, t), SPLIT_PLACE[w, m] % 2
                act.wait_ge(s_sp_ps, n + 1)
                if not isinstance(n, int) or n >= 2:
                    act.wait_ge(s_parts_out, 16 * (n - 1))
                nc.scalar.activation(parts[b][:, 0, :], side_ps[at][:, :], ACT.Copy,
                                     scale=SCALE if w in (QS, QX) else 1.0).then_inc(s_hi, 1)

            def gate_tanh(t, k, at):
                act.wait_ge(s_gu_ps, 2 * NHID * t + k + 1)
                nc.scalar.activation(gate[k % 2], side_ps[at][:, 0:T // 2], ACT.Tanh, scale=W_SCALE / 2).then_inc(s_tanh, 1)

            def hidden_high(t, k):
                act.wait_ge(s_hid, 2 * NHID * t + k + 1)
                nc.scalar.copy(hid[0][:, k % NHID, :], hid32[k % 2]).then_inc(s_hhi, 1)

            def side_work(u, t, g, name, tt):
                (kind, m), at = kind_no(name), side_bank(u, g, name)
                if kind == "mt":
                    max_rows(*next_job(u, t, g), at)
                elif kind == "xt":
                    act.wait_ge(s_xt_ps, KC * tt + m + 1)
                    nc.scalar.copy(aT[0][:, m, :], side_ps[at][:, :]).then_inc(s_xhi, 1)
                elif kind == "yt":
                    act.wait_ge(s_yt_ps, KC * tt + m + 1)
                    nc.scalar.copy(aT[0][:, m, :], side_ps[at][:, :]).then_inc(s_yhi, 1)
                elif kind in ("qs", "ks", "kx", "qx"):
                    high({"qs": QS, "ks": KS, "kx": KX, "qx": QX}[kind], m, tt, at)
                elif kind == "at":
                    if m == 0 and not is_at(tt, 0):
                        act.wait_ge(s_hlo, 2 * NHID * tt)
                    act.wait_ge(s_att_ps, KC * tt + m + 1)
                    nc.scalar.copy(oT[:, m, :], side_ps[at][:, :]).then_inc(s_att, 1)
                elif kind == "v":
                    act.wait_ge(s_v_ps, 2 * tt + m + 1)
                    nc.scalar.copy(V[S][:, 2 * m:2 * m + 2, :, 0:HD],
                                   side_ps[at][:, :].rearrange("p (c h d) -> p c h d", c=2, d=HD)).then_inc(s_v, 1)
                elif kind == "gu":
                    gate_tanh(tt, m, at)

            def side_work_after(u, t, g, name, tt):
                kind, m = kind_no(name)
                if kind == "mt":
                    max_rows_load(*next_job(u, t, g))
                elif kind == "gu":
                    hidden_high(tt, m)

            def attention(u, t, trailing):
                for g in range(NG):
                    for kt in range(NT):
                        wd = width(u, kt)
                        before = NT * job(u, t, g) + kt - 1
                        if not (isinstance(before, int) and before <= 0):
                            act.wait_ge(s_pv, before)
                        for end, cs in enumerate(halves(u, kt)):
                            for c, heads in cs:
                                act.wait_ge(s_score, exp_no(u, t, g, c) + 1)
                                src = score_ps[score_bank(u, g, c)][:, 0:wd * len(heads)].rearrange("p (h c) -> p h c", c=wd)
                                nc.scalar.activation(P[kt % 2][:, heads[0]:heads[-1] + 1, 0:wd], src, ACT.Exp).then_inc(s_exp, 1)
                            for name, gg in beside(u, t, g, kt, end, back=1):
                                side_work_after(u, t, gg, name, sequence(u, name, t))
                            if trailing and kt == 0 and end:
                                pv_out(*trailing)
                            for name, _ in beside(u, t, g, kt, end):
                                side_work(u, t, g, name, sequence(u, name, t))
                    trailing = (u, t, g)
                for name, g in beside(u, t, NG - 1, NT - 1, 1):
                    side_work_after(u, t, g, name, sequence(u, name, t))
                return trailing

            def first_rows(u, t, g, at):
                max_rows(u, t, g, at)
                max_rows_load(u, t, g)

            for name in FIRST:
                side_work(X, -2, 0, name, 0)
            first_rows(S, 0, 0, 0)
            act.wait_ge(s_w_set, 5)
            trailing = attention(S, 0, None)
            pv_out(*trailing)
            for name in LINK:
                side_work(X, -1, 0, name, sequence(X, name, -1))
            first_rows(S, 1, 0, 0)
            attention(S, 1, None)
            with act.Fori(0, LAST - 1) as t:
                trailing = attention(X, t, (S, t + 1, NG - 1))
                attention(S, t + 2, trailing)
            trailing = attention(X, LAST - 1, (S, LAST, NG - 1))
            pv_out(*trailing)
            for n, name in enumerate(FFN):
                side_work(S, LAST + 1, 0, name, LAST - 1)
                if n:
                    side_work_after(S, LAST + 1, 0, FFN[n - 1], LAST - 1)
                if n == 1:
                    first_rows(X, LAST, 0, 1)
            trailing = attention(X, LAST, None)
            pv_out(*trailing)
            for n, name in enumerate(FFN):
                side_work(S, LAST + 2, 0, name, LAST)
                if n:
                    side_work_after(S, LAST + 2, 0, FFN[n - 1], LAST)

        @block.vector
        def _(dve):
            def norm(i, src, t, tiles=range(NT)):
                for c in tiles:
                    nc.vector.bn_stats(stats[:, c, :], src[:, c, :]).then_inc(s_stat[i], 1)
                if tiles[-1] == NT - 1:
                    for c in range(NT):
                        wait_apart(dve, s_stat[i], NT * t + c + 1)
                        nc.vector.bn_aggr(mv[:, c, :], stats[:, c, :]).then_inc(s_aggr[i], 1)

            def norm_end(i, src, t, tiles=range(NT)):
                if tiles[0] == 0:
                    dve.wait_ge(s_rstd[i], t + 1)
                for c in tiles:
                    nc.vector.tensor_scalar(ln[:, c, :], src[:, c, :], mv[:, c, 0:1], rstd[:, c:c + 1],
                                            ALU.subtract, ALU.mult).then_inc(s_ln[i], 1)

            def take_max(u, t, g, i):
                keys = 128 * (i % NT + 1) if u == S else T
                dve.wait_ge(s_max_ps, max_no(u, t, g, i) + 1)
                nc.vector.tensor_reduce(mx[g % 2][:, i % NT, i // NT:i // NT + 1], max_ps[max_bank(i)][:, 0:keys], AX.X,
                                        ALU.max, negate=True).then_inc(s_max, 1)

            def low(m, t, at, sem_hi, sem_lo):
                dve.wait_ge(sem_hi, KC * t + m + 1)
                nc.vector.tensor_tensor(aT[1][:, m, :], side_ps[at][:, :], aT[0][:, m, :].bitcast(f32), ALU.subtract).then_inc(sem_lo, 1)

            def left_over(w, m, t, at):
                n, b = split_no(w, m, t), SPLIT_PLACE[w, m] % 2
                dve.wait_ge(s_hi, n + 1)
                nc.vector.scalar_tensor_tensor(rest[b][:, :], side_ps[at][:, :], SCALE if w in (QS, QX) else 1.0,
                                               parts[b][:, 0, :], ALU.mult, ALU.subtract).then_inc(s_rest, 1)

            def head_outputs(u, t, g, at):
                j = job(u, t, g)
                dve.wait_ge(s_ot_ps, j + 1)
                src = side_ps[at][:, :].rearrange("p (c h e) -> p c h e", c=NT, h=GH)
                nc.vector.reciprocal(rden[g % 2][:, :, :], src[:, :, :, HD]).then_inc(s_rden, 1)
                dve.wait_ge(s_rden, j + 1)
                to = att[:, :, HD * GH * g:HD * GH * (g + 1)].rearrange("p c (h d) -> p c h d", d=HD)
                nc.vector.tensor_tensor(to, src[:, :, :, 0:HD], rden[g % 2][:, :, :].unsqueeze(3).broadcast_to([128, NT, GH, HD]),
                                        ALU.mult).then_inc(s_ot, 1)

            def add_wo(t, half, at):
                dve.wait_ge(s_again, 16 * (t + 1))
                dve.wait_ge(s_wo_ps, 2 * t + half + 1)
                rows = x1[:, 2 * half:2 * half + 2, :]
                nc.vector.tensor_tensor(rows, side_ps[at][:, :].rearrange("p (c d) -> p c d", c=2), rows, ALU.add).then_inc(s_x1, 1)

            def add_att(t):
                dve.wait_ge(s_ot, job(X, t, NG - 1) + 1)
                dve.wait_ge(s_moved, t + 1)
                nc.vector.tensor_tensor(x2[:, :, :], x2[:, :, :], att[:, :, :], ALU.add).then_inc(s_x2, 1)

            def hidden(t, k, at):
                n = 2 * NHID * t + k
                if k % NHID >= 2:
                    dve.wait_ge(s_hlo, 2 * NHID + n - 1)
                dve.wait_ge(s_tanh, n + 1)
                nc.vector.scalar_tensor_tensor(gate[k % 2], gate[k % 2], 1.0, side_ps[at][:, 0:T // 2],
                                               ALU.add, ALU.mult).then_inc(s_gate, 1)
                dve.wait_ge(s_gate, n + 1)
                nc.vector.tensor_tensor(hid32[k % 2], side_ps[at][:, T // 2:T], gate[k % 2], ALU.mult).then_inc(s_hid, 1)

            def output(t, r, at):
                dve.wait_ge(s_dn_ps, NT * t + r + 1)
                nc.vector.scalar_tensor_tensor(x2[:, r, :], side_ps[at][:, 0:D], W_SCALE ** 3 / 2, x2[:, r, :],
                                               ALU.mult, ALU.add).then_inc(s_y, 1)

            def side_work(u, t, g, name, tt):
                (kind, m), at = kind_no(name), side_bank(u, g, name)
                if kind == "ot":
                    head_outputs(*prev_job(u, t, g), at)
                elif kind in ("qs", "ks", "kx", "qx"):
                    left_over({"qs": QS, "ks": KS, "kx": KX, "qx": QX}[kind], m, tt, at)
                elif kind == "xt":
                    low(m, tt, at, s_xhi, s_xt)
                elif kind == "yt":
                    low(m, tt, at, s_yhi, s_yt)
                elif kind == "wo":
                    add_wo(tt, m, at)
                elif kind == "gu":
                    hidden(tt, m, at)
                elif kind == "dn":
                    output(tt, m, at)

            def norm_step(u, t, g, kt, end):
                place, low_rows, high_rows = (u, g, kt, end), range(NT // 2), range(NT // 2, NT)
                if u == X and not (isinstance(t, int) and t >= LAST - 1):
                    if place == (X, 0, 0, 0):
                        dve.wait_ge(s_x, 16 * (t + 3))
                        norm(0, x_in, t + 2, low_rows)
                    elif place == (X, 0, 0, 1):
                        norm(0, x_in, t + 2, high_rows)
                    elif place == (X, 0, 1, 1):
                        dve.wait_ge(s_hlo, 2 * NHID * (t + 1))
                        norm_end(0, x_in, t + 2, low_rows)
                    elif place == (X, 0, 2, 0):
                        norm_end(0, x_in, t + 2, high_rows)
                if u == X and not is_at(t, LAST):
                    if place == (X, 1, 3, 0):
                        dve.wait_ge(s_x1, 2 * (t + 2))
                        norm(1, x1, t + 1, low_rows)
                    elif place == (X, 1, 3, 1):
                        norm(1, x1, t + 1, high_rows)
                    elif place == (X, 2, 0, 1):
                        norm_end(1, x1, t + 1, low_rows)
                    elif place == (X, 2, 1, 0):
                        norm_end(1, x1, t + 1, high_rows)
                if u == S and not (isinstance(t, int) and t <= 1):
                    if place == (S, 0, 2, 0):
                        add_att(t - 2)
                    elif place == (S, 0, 2, 1):
                        dve.wait_ge(s_x2, t - 1)
                        norm(2, x2, t - 2, low_rows)
                    elif place == (S, 0, 3, 0):
                        norm(2, x2, t - 2, high_rows)
                    elif place == (S, 0, 3, 1):
                        norm_end(2, x2, t - 2, low_rows)
                    elif place == (S, 1, 0, 0):
                        norm_end(2, x2, t - 2, high_rows)
                if u == S and is_at(t, 0):
                    if place == (S, 2, 0, 1):
                        dve.wait_ge(s_x, 16 * 2)
                        norm(0, x_in, 1)
                    elif place == (S, 3, 0, 1):
                        norm_end(0, x_in, 1)

            def cross_out(t):
                add_att(t)
                dve.wait_ge(s_x2, t + 1)
                norm(2, x2, t)

            def attention(u, t):
                for g in range(NG):
                    ahead = max_job(u, t, g)
                    for kt in range(NT):
                        for end in range(2):
                            if ahead:
                                take_max(*ahead, 4 * kt + 2 * end)
                            for name, gg in beside(u, t, g, kt, end, back=1):
                                side_work(u, t, gg, name, sequence(u, name, t))
                            if ahead:
                                take_max(*ahead, 4 * kt + 2 * end + 1)
                            norm_step(u, t, g, kt, end)
                for name, g in beside(u, t, NG - 1, NT - 1, 1):
                    side_work(u, t, g, name, sequence(u, name, t))

            def split_weights(n, w_in, w_sb, k0, k1):
                nc.vector.tensor_copy(w_sb[0][:, k0:k1, :], w_in).then_inc(s_whi, 1)
                dve.wait_ge(s_whi, n + 1)
                nc.vector.tensor_tensor(w_sb[1][:, k0:k1, :], w_in, w_sb[0][:, k0:k1, :].bitcast(f32),
                                        ALU.subtract).then_inc(s_w_set, 1)

            dve.sem_inc(s_y, NT)
            dve.sem_inc(s_out, 16)

            dve.wait_ge(s_x, 16)
            norm(0, x_in, 0)
            norm_end(0, x_in, 0)
            dve.wait_ge(s_w, 16 * 4)
            for n, (w_in, w_sb) in enumerate(((wq_in, Wq), (wk_in, Wk), (wv_in, Wv))):
                split_weights(n, w_in, w_sb, 0, KC)
            for name in FIRST:
                side_work(X, -2, 0, name, 0)
            for n, (w_in, w_sb, k0, k1) in enumerate(((wg_in, Wg, 0, KC), (wu_in, Wu, 0, KC), (wd_in[0], Wd, 0, NT),
                                                      (wd_in[1], Wd, NT, NHID)), 3):
                if n == 1:
                    dve.wait_ge(s_wi, 16 * 4)
                split_weights(n, w_in, w_sb, k0, k1)
            for g in range(2):
                for i in range(GH * NT):
                    take_max(S, 0, g, i)
            attention(S, 0)
            head_outputs(S, 0, NG - 1, 0)
            for name in LINK:
                if name == "qs1":
                    norm_end(1, x1, 0)
                side_work(X, -1, 0, name, sequence(X, name, -1))
                if name == "wo1":
                    dve.wait_ge(s_x1, 2)
                    norm(1, x1, 0)
            for g in range(2):
                for i in range(GH * NT):
                    take_max(S, 1, g, i)
            attention(S, 1)
            with dve.Fori(0, LAST - 1) as t:
                attention(X, t)
                attention(S, t + 2)
            attention(X, LAST - 1)
            head_outputs(X, LAST - 1, NG - 1, 0)
            cross_out(LAST - 1)
            for i in range(GH * NT):
                take_max(X, LAST, 0, i)
            norm_end(2, x2, LAST - 1)
            for n, name in enumerate(FFN):
                side_work(S, LAST + 1, 0, name, LAST - 1)
                if n < GH * NT:
                    take_max(X, LAST, 1, n)
            attention(X, LAST)
            head_outputs(X, LAST, NG - 1, 0)
            cross_out(LAST)
            dve.wait_ge(s_hlo, 2 * NHID * B)
            norm_end(2, x2, LAST)
            for name in FFN:
                side_work(S, LAST + 2, 0, name, LAST)



def kernel(**inputs):
    import numpy as np
    import ml_dtypes
    import concourse.bacc as bacc
    from concourse.bass_utils import run_bass_kernel_spmd as run

    bf = ml_dtypes.bfloat16
    a = {k: np.asarray(v) for k, v in inputs.items()}
    B, T, D = a["x"].shape
    NH = 16

    def three_parts(v):
        parts = []
        for _ in range(3):
            parts.append(v.astype(bf))
            v = v - parts[-1].astype(np.float64)
        return np.stack(parts)

    base = 2.0 ** (-8.0 / NH)
    slopes = np.array([base ** i for i in range(1, NH + 1)], np.float32).astype(np.float64)
    ramp = three_parts(slopes[:, None] * np.arange(T))
    ramp = np.stack([ramp, np.zeros_like(ramp)])
    fill = np.ones((3, NH, T), bf)
    at = np.arange(128)
    hidden = np.where(at[:, None] < at[None, :], -1e30, 0.0)
    masks = np.stack([hidden, hidden.T, np.eye(128)], 1).astype(bf)

    arrays = {
        "x": a["x"], "ctx": a["ctx_1024"],
        "wq": a["L0_attn_Wq"].T, "wk": a["L0_attn_Wk"].T, "wv": a["L0_attn_Wv"].T, "wo": a["L0_attn_Wo"].T,
        "w_gate": a["L0_ffn_w_gate"].T, "w_up": a["L0_ffn_w_up"].T, "w_down": a["L0_ffn_w_down"].T,
        "ramp": ramp, "fill": fill, "masks": masks,
    }
    arrays = {f"{k}_dram": np.ascontiguousarray(v) for k, v in arrays.items()}
    nc = bacc.Bacc("TRN2", target_bir_lowering=False, num_devices=1)
    ins = [nc.dram_tensor(k, v.shape, mybir.dt.from_np(v.dtype), kind="ExternalInput").ap() for k, v in arrays.items()]
    parts = nc.dram_tensor("parts_dram", (4, 3, D, T), mybir.dt.bfloat16, kind="Internal").ap()
    out = nc.dram_tensor("out_dram", (B, T, D), mybir.dt.float32, kind="ExternalOutput").ap()
    decoder_kernel(nc, *ins, parts, out)
    r = run(nc, [arrays], core_ids=[0])
    return r.results[0]["out_dram"]
```

```python
import concourse.bass as bass
from concourse import mybir
from contextlib import ExitStack


def decoder_kernel(nc, x, ctx, wq, wk, wv, wo, w_gate, w_up, w_down, ramp, fill, masks, parts_dram, out):
    f32, bf16, f32r, i32 = mybir.dt.float32, mybir.dt.bfloat16, mybir.dt.float32r, mybir.dt.int32
    ALU, ACT, AX = mybir.AluOpType, mybir.ActivationFunctionType, mybir.AxisListType

    B, T, D = x.shape
    HD = 16
    NH = D // HD
    HID = w_gate.shape[1]
    NT = T // 128
    KC = D // 128
    NHID = HID // 128
    NG = 4
    GH = NH // NG
    HH = NH // 2
    ROWS = [(0, 0, 0, 3), (48, 0, 1, 2), (80, 0, 2, 1)]
    R_MAX = HD * 6 + 3
    R_ALL = R_MAX + 3
    S, X = 0, 1
    QS, KS, KX, QX = 0, 1, 2, 3
    SCALE = HD ** -0.5
    EPS = 1e-5
    W_SCALE = 1.0 / 127.0
    LAST = B - 1

    def width(u, kt):
        return T - 128 * kt if u == S else T

    def chunks(u, kt):
        n = max(1, 512 // width(u, kt))
        return [list(range(i, i + n)) for i in range(0, GH, n)]

    def halves(u, kt):
        cs = list(enumerate(chunks(u, kt), sum(len(chunks(u, k)) for k in range(kt))))
        return cs[:(len(cs) + 1) // 2], cs[(len(cs) + 1) // 2:]

    EXPS = [sum(len(chunks(u, kt)) for kt in range(NT)) for u in (S, X)]
    RING, MAX_RING = 2, 3

    def score_bank(u, g, c):
        return (NG * EXPS[S] * u + EXPS[u] * g + c) % RING

    def max_bank(g, i):
        return (GH * NT * g + i) % MAX_RING

    def is_at(t, value):
        return isinstance(t, int) and t == value

    def self_before(u, t):
        return t if u == S else B if is_at(t, LAST) else t + 2

    def cross_before(u, t):
        return t if u == X else 0 if is_at(t, 0) else t - 1

    def job(u, t, g):
        return NG * (self_before(u, t) + cross_before(u, t)) + g

    def exp_no(u, t, g, c):
        return NG * EXPS[S] * self_before(u, t) + NG * EXPS[X] * cross_before(u, t) + EXPS[u] * g + c

    def max_no(u, t, g, i):
        return GH * NT * job(u, t, g) + i

    SPLIT_PLACE = {(QS, 0): 0, (KS, 0): 1, (QS, 1): 2, (KS, 1): 3, (KX, 0): 4, (QX, 0): 5, (QX, 1): 6, (KX, 1): 7}

    def part_place(w, part):
        return part if w in (QS, QX) else 2 - part

    def split_no(w, m, t):
        place = SPLIT_PLACE[w, m]
        if w in (QS, KS):
            return place if is_at(t, 0) else 8 * t - 4 + place
        return 8 * t + place if is_at(t, LAST) else 8 * t + 4 + place

    FIRST, NEXT, FINAL = "first", "next to last", "final"

    BESIDE = {
        (X, 0): [("", ""), ("mt", "ot"), ("", "xt0"), ("xt1", "qs0")],
        (X, 1): [("ks0", "at0"), ("mt at1", "ot"), ("wo0", "wo1"), ("qs1", "ks1")],
        (X, 2): [("v0", "v1"), ("mt", "ot"), ("kx0", ""), ("", "")],
        (X, 3): [("qx0", ""), ("mt", "ot"), ("qx1", ""), ("kx1", "")],
        (S, 0): [("", ""), ("mt", "ot"), ("", ""), ("", "")],
        (S, 1): [("", "yt0"), ("yt1 mt", "ot"), ("gu0", "gu1"), ("gu2", "gu3")],
        (S, 2): [("gu4", "gu5"), ("mt", "ot"), ("", "dn0 dn1"), ("gu6", "gu7")],
        (S, 3): [("gu8", "gu9"), ("gu10 mt", "ot"), ("gu11", ""), ("", "dn2 dn3")],
        (FIRST, 0): [("", ""), ("mt", ""), ("", ""), ("", "")],
        (FIRST, 1): [("", ""), ("mt", "ot"), ("", ""), ("", "")],
        (FIRST, 2): [("xt0", "xt1"), ("mt", "qs0"), ("ot", "ks0"), ("", "")],
        (FIRST, 3): [("", ""), ("", "ot"), ("", ""), ("", "")],
        (FINAL, 0): [("gu2", "gu3"), ("mt", "gu4"), ("gu5", ""), ("dn0", "dn1")],
        (FINAL, 1): [("gu6", "gu7"), ("mt", "ot"), ("gu8", "gu9"), ("gu10", "")],
        (FINAL, 2): [("gu11", ""), ("mt", "ot"), ("", "dn2"), ("dn3", "")],
        (FINAL, 3): [("", ""), ("", "ot"), ("", ""), ("", "")],
        (NEXT, 0): [("", ""), ("mt", "ot"), ("at0", "at1"), ("wo0", "wo1")],
        (NEXT, 1): [("kx0", ""), ("mt", "ot"), ("", ""), ("qx0", "")],
        (NEXT, 2): [("qx1", ""), ("mt", "ot"), ("kx1", ""), ("", "")],
        (NEXT, 3): [("", ""), ("", "ot"), ("", ""), ("", "")],
    }
    PLACES = [(u, g, kt, end) for u in (X, S) for g in range(NG) for kt in range(NT) for end in range(2)]
    ALL = [(u, g, name) for u, g, kt, end in PLACES for name in BESIDE[u, g][kt][end].split()]

    def side_bank(u, g, name):
        if name[:2] in ("mt", "ot"):
            return ALL.index((u, g, name)) % 2
        return [n for _, _, n in ALL].index(name) % 2

    def kind_no(name):
        kind = name.rstrip("0123456789")
        return kind, int(name[len(kind):] or 0)

    def sequence(u, name, t):
        kind, _ = kind_no(name)
        if u == S and is_at(t, 0):
            return 1
        if u == X and is_at(t, LAST):
            return LAST - 1
        return {"xt": t + 2, "qs": t + 2, "ks": t + 2, "v": t + 2, "at": t + 1, "wo": t + 1, "kx": t + 1, "qx": t + 1,
                "yt": t - 2, "gu": t - 2, "dn": t - 2}.get(kind, t)

    def present(u, t, g, name):
        kind, _ = kind_no(name)
        return not (u == S and is_at(t, 1)) or kind == "mt" or kind == "ot" and g > 0

    def table(u, t):
        if u == S:
            return FIRST if is_at(t, 0) else S
        return FINAL if is_at(t, LAST) else NEXT if is_at(t, LAST - 1) else X

    def beside(u, t, g, kt, end, back=0):
        n = PLACES.index((u, g, kt, end)) - back
        if n < 0 or PLACES[n][0] != u:
            return []
        _, g, kt, end = PLACES[n]
        return [(name, g) for name in BESIDE[table(u, t), g][kt][end].split() if present(u, t, g, name)]

    BEFORE_FIRST = ["xt0", "xt1", "qs0", "ks0", "v0", "v1", "qs1", "ks1"]
    AFTER_FIRST = ["at0", "at1", "wo0", "wo1", "qs1", "ks1", "v0", "v1", "kx0", "qx0", "qx1", "kx1"]
    BEFORE_FINAL = ["yt0", "yt1", "gu0", "gu1"]
    AFTER_FINAL = ["yt0", "yt1"] + [f"gu{i}" for i in range(NHID + 1)] + ["dn0", "dn1"] + [
        f"gu{i}" for i in range(NHID + 1, 2 * NHID)] + ["dn2", "dn3"]
    PER_ITEM = 3
    MAXIMA_0, MAXIMA_0_LOADED = 5, 7
    FINAL_MAXIMA = [8, 8, 12, 16, 16]

    def next_job(u, t, g):
        if g < NG - 1:
            return u, t, g + 1
        if u == S:
            return (S, 1, 0) if is_at(t, 0) else (X, t - 1, 0)
        return (X, LAST, 0) if is_at(t, LAST - 1) else (S, t + 2, 0)

    def prev_job(u, t, g):
        if g:
            return u, t, g - 1
        if u == S:
            return (S, 0, NG - 1) if is_at(t, 1) else (X, t - 2, NG - 1)
        return (X, LAST - 1, NG - 1) if is_at(t, LAST) else (S, t + 1, NG - 1)

    def max_job(u, t, g):
        if g < 2:
            return u, t, g + 2
        if u == S:
            return None if is_at(t, 0) else (X, t - 1, g - 2)
        if is_at(t, LAST - 1):
            return (X, LAST, 0) if g == NG - 1 else None
        return None if is_at(t, LAST) else (S, t + 2, g - 2)

    es = ExitStack()
    with es:
        def sb(name, shape, dt=f32):
            return es.enter_context(nc.sbuf_tensor(name, shape, dt))

        def sem(name):
            return es.enter_context(nc.semaphore(name))

        LQ = [sb("lq_self", [128, NH, T], bf16), sb("lq_cross", [128, NH, T], bf16)]
        LK = [sb("lk_self", [128, NH, T], bf16), sb("lk_cross", [128, NH, T], bf16)]
        V = [sb("v_self", [128, NT, NH, 2 * HD]), sb("v_cross", [128, NT, NH, 2 * HD])]
        P = [sb(f"probs{i}", [128, GH, T]) for i in range(2)]
        x_in = sb("x_in", [128, NT, D])
        ctx_in = sb("ctx_in", [128, NT, D])
        x1 = sb("x1", [128, NT, D])
        x2 = sb("x2", [128, NT, D])
        att = sb("att", [128, NT, D])
        ln = sb("ln", [128, NT, D])
        aT = [sb(f"aT_{n}", [128, KC, T], f32r) for n in ("hi", "lo")]
        hid = [sb(f"hid_{n}", [128, NHID, T // 2], f32r) for n in ("hi", "lo")]
        flat = ln[:, :, :].rearrange("p c d -> p (c d)")
        oT = flat.rearrange("p (c t) -> p c t", c=KC)
        hid32, gate = ([flat[:, T // 2 * (2 * j + i):T // 2 * (2 * j + i + 1)] for i in range(2)] for j in range(2))
        parts = [sb(f"parts{i}", [128, 3, T], bf16) for i in range(2)]
        rest = [sb(f"rest{i}", [128, T]) for i in range(2)]
        pv_sb = sb("pv_sb", [128, T])
        mx = [sb(f"mx{i}", [128, NT, GH]) for i in range(2)]
        mxr = [sb(f"mxr{i}", [128, 2, NT, GH]) for i in range(2)]
        mxp = [sb(f"mxp{i}", [128, NT, 3, GH], bf16) for i in range(2)]
        mT = [sb(f"mT{i}", [3 * GH, T], bf16) for i in range(2)]
        rden = [sb(f"rden{i}", [128, NT, GH]) for i in range(2)]
        stats = sb("stats", [128, NT, 6])
        mv = sb("mv", [128, NT, 2])
        var_eps = sb("var_eps", [128, NT])
        rstd = sb("rstd", [128, NT])
        low_max = sb("low_max", [128, 4])
        low_any = sb("low_any", [1, 1])
        low_flag = sb("low_flag", [1, 1], i32)
        mhalf = sb("mhalf", [128, NT])
        ident = sb("ident", [128, 128])
        identb = sb("identb", [128, 128], bf16)
        maskb = sb("maskb", [128, 2, 128], bf16)
        Wo = sb("wo_sb", [128, KC, D])
        Wq, Wk, Wv = ([sb(f"w{n}_{a}", [128, KC, D], f32r) for a in ("hi", "lo")] for n in "qkv")
        Wg, Wu = ([sb(f"w{n}_{a}", [128, KC, HID], f32r) for a in ("hi", "lo")] for n in "gu")
        Wd = [sb(f"wd_{a}", [128, NHID, D], f32r) for a in ("hi", "lo")]
        wq_in, wk_in, wv_in = att[:, 0:KC, :], att[:, KC:2 * KC, :], x2[:, 0:KC, :]
        wg_in = P[0][:, :, :].rearrange("p h t -> p (h t)").bitcast(i32)[:, 0:KC * HID].rearrange("p (c n) -> p c n", c=KC)
        wu_in = P[1][:, :, :].rearrange("p h t -> p (h t)").bitcast(i32)[:, 0:KC * HID].rearrange("p (c n) -> p c n", c=KC)
        wd_in = [x1[:, :, :].bitcast(i32), x2[:, NT - (NHID - NT):NT, :].bitcast(i32)]

        score_ps = [es.enter_context(nc.psum_tensor(f"score_ps{i}", [128, 512], f32)) for i in range(RING)]
        max_ps = [es.enter_context(nc.psum_tensor(f"max_ps{i}", [128, 512], f32)) for i in range(MAX_RING)]
        pv_ps = es.enter_context(nc.psum_tensor("pv_ps", [128, 512], f32))
        side_ps = [es.enter_context(nc.psum_tensor(f"side{i}", [128, 512], f32)) for i in range(2)]

        s_const, s_w, s_wi, s_x, s_ctx, s_out = (sem(n) for n in ("const_in", "w_in", "wi_in", "x_in", "ctx_in", "out"))
        s_parts_out = sem("parts_out")
        s_rows = [[sem(f"rows_{u}{m}") for m in range(2)] for u in "sx"]
        s_mrow = [sem(f"mrow{i}") for i in range(2)]
        s_carry = sem("carries_waits")
        s_set, s_ident, s_whi, s_w_set = sem("set"), sem("identity"), sem("w_hi"), sem("w_set")
        s_low, s_low_ps = sem("low_parts"), sem("low_ps")
        s_max_ps, s_max = sem("max_ps"), sem("max_taken")
        s_mpart, s_mt_ps, s_mt = sem("max_parts"), sem("mt_ps"), sem("mt_taken")
        s_score, s_exp, s_pv, s_pvout = sem("score_ps"), sem("exp"), sem("pv_ps"), sem("pv_taken")
        s_ot_ps, s_rden, s_ot = sem("ot_ps"), sem("rden"), sem("ot_taken")
        s_sp_ps, s_hi, s_rest, s_mid, s_lo = (sem(n) for n in ("split_ps", "part_hi", "part_rest", "part_mid", "part_lo"))
        s_stat, s_aggr, s_vare, s_rstd, s_ln = ([sem(f"{n}{i}") for i in range(3)]
                                               for n in ("ln_stat", "ln_aggr", "ln_vare", "ln_rstd", "ln_done"))
        s_xt_ps, s_xhi, s_xt, s_yt_ps, s_yhi, s_yt = (sem(n) for n in ("xt_ps", "xt_hi", "xt_taken", "yt_ps", "yt_hi", "yt_taken"))
        s_v_ps, s_v, s_vx = sem("v_ps"), sem("v_taken"), sem("v_cross")
        s_att_ps, s_att, s_wo_ps, s_x1, s_x2 = (sem(n) for n in ("attT_ps", "attT_taken", "wo_ps", "x1", "x2"))
        s_again, s_moved = sem("x_again"), sem("x1_moved")
        s_gu_ps, s_tanh, s_gate, s_hid, s_hhi, s_hlo, s_dn_ps, s_y = (
            sem(n) for n in ("gate_up_ps", "tanh", "gate", "hidden", "hidden_hi", "hidden_lo", "down_ps", "y"))

        block = es.enter_context(nc.Block())

        def result(t):
            return x1 if is_at(t, LAST) else x2

        def wait_apart(engine, semaphore, value):
            engine.wait_ge(semaphore, value)
            engine.sem_inc(s_carry, 1)

        @block.sync
        def _(sp):
            def load_x(t):
                if not is_at(t, 0):
                    wait_apart(sp, s_ln[0], NT * t)
                sp.dma_start(x_in[:, :, :], x[t, :, :].rearrange("(c p) d -> p c d", p=128)).then_inc(s_x, 16)

            def load_x_again(t):
                if is_at(t, 0):
                    wait_apart(sp, s_w_set, 7)
                else:
                    wait_apart(sp, s_moved, t)
                    wait_apart(sp, s_ln[1], NT * t)
                sp.dma_start(x1[:, :, :], x[t, :, :].rearrange("(c p) d -> p c d", p=128)).then_inc(s_again, 16)

            def load_ctx(t):
                if not is_at(t, 0):
                    wait_apart(sp, s_sp_ps, split_no(KX, 1, t - 1) + 1)
                    wait_apart(sp, s_vx, t)
                sp.dma_start(ctx_in[:, :, :], ctx[t, :, :].rearrange("(c p) d -> p c d", p=128)).then_inc(s_ctx, 16)

            def split(w, m, t):
                n = split_no(w, m, t)
                sp.wait_ge(s_lo, n + 1)
                sp.dma_start(parts_dram[w, m, :, :, :].rearrange("a p c -> p a c"),
                             parts[SPLIT_PLACE[w, m] % 2][:, :, :]).then_inc(s_parts_out, 16)
                wait_apart(sp, s_parts_out, 16 * n + 16)
                if w in (QX, KX) and not is_at(t, 0):
                    wait_apart(sp, s_score, exp_no(X, t - 1, 2 * m + 1, EXPS[X] - 1) + 1)
                u = S if w in (QS, KS) else X
                for row, of_query, of_key, n_parts in ROWS:
                    to, first = (LQ[u], of_query) if w in (QS, QX) else (LK[u], of_key)
                    sp.dma_start(to[row:row + HD * n_parts, HH * m:HH * m + HH, :],
                                 parts_dram[w, m, first:first + n_parts, :, :].rearrange("a (d h) c -> (a d) h c", h=HH)
                                 ).then_inc(s_rows[u][m], 16)

            def store(t):
                sp.wait_ge(s_y, NT * (t + 2))
                sp.dma_start(out[t, :, :].rearrange("(c p) d -> p c d", p=128), result(t)[:, :, :]).then_inc(s_out, 16)

            load_x(0)
            for to, w in ((wq_in, wq), (wk_in, wk), (wv_in, wv), (Wo[:, :, :], wo)):
                sp.dma_start(to, w.rearrange("(c p) n -> p c n", p=128)).then_inc(s_w, 16)
            sp.dma_start(maskb[:, :, :], masks[:, 0:2, :]).then_inc(s_const, 16)
            sp.dma_start(identb[:, :], masks[:, 2, :]).then_inc(s_const, 16)
            for u in (S, X):
                sp.dma_start(LQ[u][R_MAX - 3:R_MAX, :, :], fill).then_inc(s_const, 16)
                sp.dma_start(LK[u][R_MAX:R_ALL, :, :], fill).then_inc(s_const, 16)
                sp.dma_start(LK[u][R_MAX - 3:R_MAX, :, :], ramp[u, :, :, :]).then_inc(s_const, 16)
            load_ctx(0)
            sp.dma_start(wg_in, w_gate.rearrange("(c p) n -> p c n", p=128)).then_inc(s_wi, 16)
            sp.dma_start(wu_in, w_up.rearrange("(c p) n -> p c n", p=128)).then_inc(s_wi, 16)
            sp.dma_start(wd_in[0], w_down[0:128 * NT, :].rearrange("(c p) n -> p c n", p=128)).then_inc(s_wi, 16)
            sp.dma_start(wd_in[1], w_down[128 * NT:HID, :].rearrange("(c p) n -> p c n", p=128)).then_inc(s_wi, 16)
            SELF, CROSS = ((QS, 0), (KS, 0), (QS, 1), (KS, 1)), ((KX, 0), (QX, 0), (QX, 1), (KX, 1))
            for w, m in SELF:
                split(w, m, 0)
            load_x(1)
            load_x_again(0)
            for w, m in SELF:
                split(w, m, 1)
            for w, m in CROSS:
                split(w, m, 0)
            load_ctx(1)
            load_x(2)

            def body(t, x_ahead=True):
                load_x_again(t + 1)
                for w, m in SELF:
                    split(w, m, t + 2)
                for w, m in CROSS:
                    split(w, m, t + 1)
                load_ctx(t + 2)
                if x_ahead:
                    load_x(t + 3)
                store(t)

            with sp.Fori(0, LAST - 2) as t:
                body(t)
            body(LAST - 2, x_ahead=False)
            load_x_again(LAST)
            for w, m in CROSS:
                split(w, m, LAST)
            store(LAST - 1)
            store(LAST)
            sp.wait_ge(s_out, 16 * (B + 1))

        @block.gpsimd
        def _(pool):
            nc.gpsimd.memset(ident[:, :], 0.0).then_inc(s_ident, 1)
            nc.gpsimd.memset(mhalf[:, :], -0.5).then_inc(s_set, 1)
            for u in (S, X):
                nc.gpsimd.memset(V[u][:, :, :, HD:2 * HD], 1.0).then_inc(s_set, 1)
            pool.wait_ge(s_ident, 1)
            nc.gpsimd.affine_select(out=ident[:, :], in_=ident[:, :], compare_op=ALU.not_equal, fill=1.0, base=0,
                                    pattern=[[-1, 128]], channel_multiplier=1).then_inc(s_ident, 1)

            def norm(i, t):
                wait_apart(pool, s_aggr[i], NT * (t + 1))
                nc.gpsimd.tensor_scalar(var_eps[:, :], mv[:, :, 1], EPS, None, ALU.add).then_inc(s_vare[i], 1)
                pool.wait_ge(s_vare[i], t + 1)
                nc.gpsimd.tensor_tensor(rstd[:, :], var_eps[:, :], mhalf[:, :], ALU.pow).then_inc(s_rstd[i], 1)

            def max_parts(u, t, g):
                j, b = job(u, t, g), g % 2
                left = mxr[b]
                wait_apart(pool, s_max, max_no(u, t, g, GH * NT - 1) + 1)
                nc.gpsimd.tensor_copy(mxp[b][:, :, 0, :], mx[b][:, :, :]).then_inc(s_mpart, 1)
                pool.wait_ge(s_mpart, 5 * j + 1)
                nc.gpsimd.tensor_tensor(left[:, 0, :, :], mx[b][:, :, :], mxp[b][:, :, 0, :], ALU.subtract).then_inc(s_mpart, 1)
                wait_apart(pool, s_mpart, 5 * j + 2)
                nc.gpsimd.tensor_copy(mxp[b][:, :, 1, :], left[:, 0, :, :]).then_inc(s_mpart, 1)
                pool.wait_ge(s_mpart, 5 * j + 3)
                nc.gpsimd.tensor_tensor(left[:, 1, :, :], left[:, 0, :, :], mxp[b][:, :, 1, :], ALU.subtract).then_inc(s_mpart, 1)
                wait_apart(pool, s_mpart, 5 * j + 4)
                nc.gpsimd.tensor_copy(mxp[b][:, :, 2, :], left[:, 1, :, :]).then_inc(s_mpart, 1)

            def split(w, m, t):
                n, b = split_no(w, m, t), SPLIT_PLACE[w, m] % 2
                if not isinstance(t, int):
                    wait_apart(pool, s_rest, n + 1)
                    nc.gpsimd.tensor_copy(parts[b][:, part_place(w, 1), :], rest[b][:, :]).then_inc(s_mid, 1)
                pool.wait_ge(s_mid, n + 1)
                nc.gpsimd.tensor_tensor(parts[b][:, part_place(w, 2), :], rest[b][:, :], parts[b][:, part_place(w, 1), :], ALU.subtract).then_inc(s_lo, 1)

            def v_cross(t):
                if not is_at(t, 0):
                    pool.wait_ge(s_pv, NT * job(X, t - 1, NG))
                wait_apart(pool, s_ctx, 16 * (t + 1))
                nc.gpsimd.tensor_copy(V[X][:, :, :, 0:HD].rearrange("p c (m h) d -> p (c m) h d", m=2),
                                      ctx_in[:, :, :].rearrange("p c (m d h) -> p (c m) h d", m=2, d=HD)).then_inc(s_vx, 1)

            def move_x1(t):
                wait_apart(pool, s_x1, 2 * (t + 1))
                wait_apart(pool, s_out, 16 * (t + 1))
                nc.gpsimd.tensor_copy(x2[:, :, :], x1[:, :, :]).then_inc(s_moved, 1)

            def hidden_low(t, k):
                pool.wait_ge(s_hhi, 2 * NHID * t + k + 1)
                nc.gpsimd.tensor_tensor(hid[1][:, k % NHID, :], hid32[k % 2], hid[0][:, k % NHID, :].bitcast(f32),
                                        ALU.subtract).then_inc(s_hlo, 1)

            def side_work(name, t):
                kind, m = kind_no(name)
                if kind in ("qs", "ks", "kx", "qx"):
                    split({"qs": QS, "ks": KS, "kx": KX, "qx": QX}[kind], m, t)
                elif kind == "gu":
                    hidden_low(t, m)

            def attention(u, t):
                for g in range(NG):
                    for kt in range(NT):
                        for end in range(2):
                            for name, _ in beside(u, t, g, kt, end, back=1):
                                side_work(name, sequence(u, name, t))
                        if (u, g, kt) == (X, 0, 0) and not (isinstance(t, int) and t >= LAST - 1):
                            norm(0, t + 2)
                        if (u, g, kt) == (X, 0, 0) and not is_at(t, LAST):
                            move_x1(t)
                        if (u, g, kt) == ((X, 1, 0) if is_at(t, LAST - 1) else (X, 1, 3)) and not is_at(t, LAST):
                            norm(1, t + 1)
                        if (u, g, kt) == (S, 0, 3) and not (isinstance(t, int) and t <= 1):
                            norm(2, t - 2)
                        if (u, g, kt) == (S, 2, 0) and not (isinstance(t, int) and t <= 1):
                            v_cross(t - 1)
                        if (u, g, kt) == (S, 0, 2) and is_at(t, 0):
                            v_cross(0)
                        if (u, g, kt) == (S, 1, 1) and is_at(t, 0):
                            norm(0, 1)
                    ahead = max_job(u, t, g)
                    if ahead:
                        max_parts(*ahead)
                for name, _ in beside(u, t, NG - 1, NT - 1, 1):
                    side_work(name, sequence(u, name, t))

            pool.sem_inc(s_hlo, 2 * NHID)
            pool.wait_ge(s_set, 1)
            norm(0, 0)
            for name in BEFORE_FIRST:
                side_work(name, 0)
            max_parts(S, 0, 0)
            max_parts(S, 0, 1)
            attention(S, 0)
            for n, name in enumerate(AFTER_FIRST):
                side_work(name, sequence(X, name, -1))
                if name == "wo1":
                    norm(1, 0)
                if n == MAXIMA_0:
                    max_parts(S, 1, 0)
            max_parts(S, 1, 1)
            attention(S, 1)
            with pool.Fori(0, LAST - 1) as t:
                attention(X, t)
                attention(S, t + 2)
            attention(X, LAST - 1)
            norm(2, LAST - 1)
            v_cross(LAST)
            for name in BEFORE_FINAL:
                side_work(name, LAST - 1)
            max_parts(X, LAST, 1)
            attention(X, LAST)
            norm(2, LAST)
            for name in AFTER_FINAL:
                side_work(name, LAST)

        @block.tensor
        def _(pe):
            class Bank:
                def __init__(self):
                    self.free = None

                def take(self, free):
                    if self.free:
                        pe.wait_ge(*self.free)
                    self.free = free

            pv_bank = Bank()
            score_banks, max_banks, side_banks = ([Bank() for _ in range(n)] for n in (RING, MAX_RING, 2))

            def transpose4(src, m, at, sem_to, free):
                ps = side_ps[at]
                side_banks[at].take(free)
                for c in range(NT):
                    last = nc.tensor.transpose(ps[:, 128 * c:128 * c + 128], src[:, c, 128 * m:128 * m + 128], ident[:, :])
                last.then_inc(sem_to, 1)

            def passes(to, a, b, where_a, where_b, k, n, terms):
                for i, (x, y) in enumerate(terms):
                    last = nc.tensor.matmul(to, a[x][where_a], b[y][where_b], start=k == i == 0, stop=k == n - 1 and i == len(terms) - 1)
                return last

            ALL_TERMS = ((0, 0), (0, 1), (1, 0))
            GATE_UP = {True: ALL_TERMS, False: ((0, 0), (0, 1))}
            DOWN = {True: ALL_TERMS, False: ((0, 0), (1, 0))}

            def bank_state():
                return [(bank, bank.free) for bank in [pv_bank] + score_banks + max_banks + side_banks]

            def project(w_sb, m, t, at, sem_to, free):
                side_banks[at].take(free)
                pe.wait_ge(s_xt, KC * (t + 1))
                for k in range(KC):
                    last = passes(side_ps[at][:, :], w_sb, aT, (slice(None), k, slice(128 * m, 128 * m + 128)),
                                        (slice(None), k, slice(None)), k, KC, ALL_TERMS)
                last.then_inc(sem_to, 1)

            def values(half, t, at):
                side_banks[at].take((s_v, 2 * t + half + 1))
                for c in range(2):
                    r = 2 * half + c
                    for k in range(KC):
                        last = passes(side_ps[at][:, 256 * c:256 * c + 256], aT, Wv,
                                            (slice(None), k, slice(128 * r, 128 * r + 128)), (slice(None), k, slice(None)), k, KC, ALL_TERMS)
                last.then_inc(s_v_ps, 1)

            def out_projection(half, t, at):
                ps = side_ps[at]
                side_banks[at].take((s_x1, 2 * t + half + 1))
                pe.wait_ge(s_att, KC * (t + 1))
                for c in range(2):
                    r = 2 * half + c
                    for k in range(KC):
                        last = nc.tensor.matmul(ps[:, 256 * c:256 * c + 256], oT[:, k, 128 * r:128 * r + 128],
                                                Wo[:, k, :], start=k == 0, stop=k == KC - 1)
                last.then_inc(s_wo_ps, 1)

            def max_transposes(u, t, g, at):
                j = job(u, t, g)
                side_banks[at].take((s_mt, j + 1))
                pe.wait_ge(s_mpart, 5 * j + 5)
                for c in range(NT):
                    last = nc.tensor.transpose(side_ps[at][:, :].bitcast(bf16)[0:3 * GH, 128 * c:128 * c + 128],
                                               mxp[g % 2][:, c, :, :].rearrange("p a h -> p (a h)"), identb[:, :])
                last.then_inc(s_mt_ps, 1)

            def out_transposes(u, t, g, at):
                j = job(u, t, g)
                side_banks[at].take((s_ot, j + 1))
                pe.wait_ge(s_pvout, j + 1)
                for c in range(NT):
                    last = nc.tensor.transpose(side_ps[at][:, 128 * c:128 * c + 128], pv_sb[:, 128 * c:128 * c + 128], ident[:, :])
                last.then_inc(s_ot_ps, 1)

            def gate_up(t, k, at, low_parts):
                half, i = k // NHID, k % NHID
                side_banks[at].take((s_hid, 2 * NHID * t + k + 1))
                pe.wait_ge(s_yt, KC * (t + 1))
                for j, w_sb in enumerate((Wg, Wu)):
                    for k in range(KC):
                        last = passes(side_ps[at][:, 256 * j:256 * j + 256], w_sb, aT,
                                            (slice(None), k, slice(128 * i, 128 * i + 128)),
                                            (slice(None), k, slice(256 * half, 256 * half + 256)), k, KC, GATE_UP[low_parts])
                last.then_inc(s_gu_ps, 1)

            def down(t, r, at, low_parts):
                side_banks[at].take((s_y, NT * (t + 1) + r + 1))
                pe.wait_ge(s_hlo, NHID * (2 * t + 2 + r // 2 + 1))
                for k in range(NHID):
                    last = passes(side_ps[at][:, 0:256], hid, Wd, (slice(None), k, slice(128 * (r % 2), 128 * (r % 2) + 128)),
                                        (slice(None), k, slice(None)), k, NHID, DOWN[low_parts])
                last.then_inc(s_dn_ps, 1)

            def side_work(u, t, g, name, tt, low_parts=True):
                (kind, m), at = kind_no(name), side_bank(u, g, name)
                if kind == "mt":
                    max_transposes(*next_job(u, t, g), at)
                elif kind == "ot":
                    out_transposes(*prev_job(u, t, g), at)
                elif kind == "xt":
                    pe.wait_ge(s_ln[0], NT * (tt + 1))
                    transpose4(ln, m, at, s_xt_ps, (s_xt, KC * tt + m + 1))
                elif kind == "yt":
                    pe.wait_ge(s_ln[2], NT * (tt + 1))
                    transpose4(ln, m, at, s_yt_ps, (s_yt, KC * tt + m + 1))
                elif kind in ("qs", "ks"):
                    w = QS if kind == "qs" else KS
                    project(Wq if w == QS else Wk, m, tt, at, s_sp_ps, (s_rest, split_no(w, m, tt) + 1))
                elif kind == "kx":
                    pe.wait_ge(s_ctx, 16 * (tt + 1))
                    transpose4(ctx_in, m, at, s_sp_ps, (s_rest, split_no(KX, m, tt) + 1))
                elif kind == "qx":
                    pe.wait_ge(s_ln[1], NT * (tt + 1))
                    transpose4(ln, m, at, s_sp_ps, (s_rest, split_no(QX, m, tt) + 1))
                elif kind == "at":
                    pe.wait_ge(s_ot, job(S, tt, NG - 1) + 1)
                    transpose4(att, m, at, s_att_ps, (s_att, KC * tt + m + 1))
                elif kind == "wo":
                    out_projection(m, tt, at)
                elif kind == "v":
                    values(m, tt, at)
                elif kind == "gu":
                    gate_up(tt, m, at, low_parts)
                else:
                    down(tt, m, at, low_parts)

            def max_product(u, t, g, i):
                n, b = max_no(u, t, g, i), max_bank(g, i)
                h, r = GH * g + i // NT, i % NT
                if i == 0 and g % 2 == 0:
                    pe.wait_ge(s_rows[u][g // 2], 16 * 6 * (t + 1))
                max_banks[b].take((s_max, n + 1))
                keys = 128 * (r + 1) if u == S else T
                last = nc.tensor.matmul(max_ps[b][:, 0:keys], LQ[u][0:R_MAX, h, 128 * r:128 * r + 128],
                                        LK[u][0:R_MAX, h, 0:keys], start=True, stop=u == X)
                if u == S:
                    last = nc.tensor.matmul(max_ps[b][:, keys - 128:keys], identb[:, :], maskb[:, 0, :],
                                            start=False, stop=True)
                last.then_inc(s_max_ps, 1)

            def scores(u, t, g, kt, c, heads):
                b, wd = score_bank(u, g, c), width(u, kt)
                score_banks[b].take((s_exp, exp_no(u, t, g, c) + 1))
                for i, hh in enumerate(heads):
                    h = GH * g + hh
                    last = nc.tensor.matmul(score_ps[b][:, wd * i:wd * i + wd], LK[u][0:R_ALL, h, 128 * kt:128 * kt + 128],
                                            LQ[u][0:R_ALL, h, T - wd:T], start=True, stop=u == X)
                    if u == S:
                        last = nc.tensor.matmul(score_ps[b][:, wd * i:wd * i + 128], identb[:, :], maskb[:, 1, :],
                                                start=False, stop=True)
                last.then_inc(s_score, 1)

            def weigh(u, t, g, kt):
                if kt == 0:
                    pv_bank.take((s_pvout, job(u, t, g) + 1))
                pe.wait_ge(s_exp, exp_no(u, t, g, sum(len(chunks(u, k)) for k in range(kt + 1)) - 1) + 1)
                wd = width(u, kt)
                for hh in range(GH):
                    last = nc.tensor.matmul(pv_ps[32 * hh:32 * hh + 32, T - wd:T], V[u][:, kt, GH * g + hh, :],
                                            P[kt % 2][:, hh, 0:wd], start=kt == 0, stop=kt == NT - 1)
                last.then_inc(s_pv, 1)

            def attention(u, t, trailing, low_parts=True):
                for g in range(NG):
                    pe.wait_ge(s_mrow[g % 2], 48 * (NG // 2 * (self_before(u, t) + cross_before(u, t)) + g // 2 + 1))
                    ahead = max_job(u, t, g)
                    for kt in range(NT):
                        if u == S and g == 0 and kt == 0:
                            pe.wait_ge(s_v, 2 * (t + 1))
                        if u == X and g == 0 and kt == 0:
                            pe.wait_ge(s_vx, t + 1)
                        for end, cs in enumerate(halves(u, kt)):
                            for i, (c, heads) in enumerate(cs):
                                scores(u, t, g, kt, c, heads)
                                if ahead and i == 0:
                                    max_product(*ahead, 4 * kt + 2 * end)
                            if ahead and not cs:
                                max_product(*ahead, 4 * kt + 2 * end)
                            if end:
                                if trailing:
                                    weigh(*trailing)
                                if ahead:
                                    max_product(*ahead, 4 * kt + 3)
                            if ahead and not end:
                                max_product(*ahead, 4 * kt + 1)
                            for name, _ in beside(u, t, g, kt, end):
                                side_work(u, t, g, name, sequence(u, name, t), low_parts)
                        trailing = (u, t, g, kt)
                return trailing

            def loop_entry(t):
                for bank in side_banks:
                    bank.free = (s_y, NT * (t + 1))
                for i in range(GH * NT - MAX_RING, GH * NT):
                    max_banks[max_bank(1, i)].free = (s_max, max_no(X, t, 1, i) + 1)
                pv_bank.free = (s_pvout, job(X, t, 0))
                for c in range(EXPS[S] - RING, EXPS[S]):
                    score_banks[score_bank(S, NG - 1, c)].free = (s_exp, exp_no(S, t + 1, NG - 1, c) + 1)

            pe.wait_ge(s_ident, 2)
            pe.wait_ge(s_const, 16 * 8)
            pe.wait_ge(s_w, 16 * 4)
            pe.wait_ge(s_set, 3)
            for name in BEFORE_FIRST:
                if name in ("qs0", "v0"):
                    pe.wait_ge(s_w_set, 2 if name == "qs0" else 3)
                side_work(X, -2, 0, name, 0)
            for g in range(2):
                for i in range(GH * NT):
                    max_product(S, 0, g, i)
                if g == 0:
                    max_transposes(S, 0, 0, 0)
            trailing = attention(S, 0, None)
            weigh(*trailing)
            out_transposes(S, 0, NG - 1, 0)
            side_banks[1].take((s_low, 5))
            pe.wait_ge(s_low, 4)
            nc.tensor.transpose(side_ps[1][0:1, 0:128], low_max[:, 3:4], ident[:, :]).then_inc(s_low_ps, 1)
            for n, name in enumerate(AFTER_FIRST):
                side_work(X, -1, 0, name, sequence(X, name, -1))
                for i in range(PER_ITEM * n, min(PER_ITEM * (n + 1), 2 * GH * NT)):
                    max_product(S, 1, i // (GH * NT), i % (GH * NT))
                if n == MAXIMA_0_LOADED:
                    max_transposes(S, 1, 0, 0)
            trailing = attention(S, 1, None)
            pe.wait_ge(s_ot, job(S, 1, NG - 2) + 1)
            pe.wait_ge(s_mt, job(X, 0, 0) + 1)
            pe.wait_ge(s_w_set, 7)
            pe.wait_ge(s_low, 6)
            no_low_parts = pe.value_load(low_flag[0:1, 0:1]) == 0

            def both_ways(work):
                state = bank_state()
                with pe.If(no_low_parts):
                    work(False)
                for bank, free in state:
                    bank.free = free
                with pe.Else():
                    work(True)

            with pe.Fori(0, LAST - 1) as t:
                loop_entry(t)
                trailing = attention(X, t, (S, t + 1, NG - 1, NT - 1))
                both_ways(lambda low_parts: attention(S, t + 2, trailing, low_parts))
            loop_entry(LAST - 1)
            trailing = attention(X, LAST - 1, (S, LAST, NG - 1, NT - 1))
            weigh(*trailing)
            out_transposes(X, LAST - 1, NG - 1, 0)
            max_transposes(X, LAST, 0, 1)

            def final(low_parts):
                for i in range(FINAL_MAXIMA[0]):
                    max_product(X, LAST, 1, i)
                for n, name in enumerate(BEFORE_FINAL):
                    side_work(S, LAST + 1, 0, name, LAST - 1, low_parts)
                    for i in range(FINAL_MAXIMA[n], FINAL_MAXIMA[n + 1]):
                        max_product(X, LAST, 1, i)
                trailing = attention(X, LAST, None, low_parts)
                weigh(*trailing)
                out_transposes(X, LAST, NG - 1, 0)
                for name in AFTER_FINAL:
                    side_work(S, LAST + 2, 0, name, LAST, low_parts)

            both_ways(final)

        @block.scalar
        def _(act):
            def max_rows(u, t, g, at):
                act.wait_ge(s_mt_ps, job(u, t, g) + 1)
                nc.scalar.copy(mT[g % 2][:, :], side_ps[at][:, :].bitcast(bf16)[0:3 * GH, 0:T]).then_inc(s_mt, 1)

            def max_rows_load(u, t, g):
                act.wait_ge(s_mt, job(u, t, g) + 1)
                for a in range(3):
                    act.dma_start(LQ[u][R_MAX + a:R_MAX + a + 1, GH * g:GH * g + GH, :],
                                  mT[g % 2][GH * a:GH * a + GH, :]).then_inc(s_mrow[g % 2], 16)

            def pv_out(u, t, g):
                j = job(u, t, g)
                act.wait_ge(s_pv, NT * (j + 1))
                nc.scalar.copy(pv_sb[:, :], pv_ps[:, :]).then_inc(s_pvout, 1)

            def high(w, m, t, at):
                n, b = split_no(w, m, t), SPLIT_PLACE[w, m] % 2
                act.wait_ge(s_sp_ps, n + 1)
                if not isinstance(n, int) or n >= 2:
                    act.wait_ge(s_parts_out, 16 * (n - 1))
                nc.scalar.activation(parts[b][:, part_place(w, 0), :], side_ps[at][:, :], ACT.Copy,
                                     scale=SCALE if w in (QS, QX) else 1.0).then_inc(s_hi, 1)

            def gate_tanh(t, k, at):
                act.wait_ge(s_gu_ps, 2 * NHID * t + k + 1)
                nc.scalar.activation(gate[k % 2], side_ps[at][:, 0:T // 2], ACT.Tanh, scale=W_SCALE / 2).then_inc(s_tanh, 1)

            def hidden_high(t, k):
                if k == NHID:
                    act.wait_ge(s_dn_ps, NT * t + 2)
                act.wait_ge(s_hid, 2 * NHID * t + k + 1)
                nc.scalar.copy(hid[0][:, k % NHID, :], hid32[k % 2]).then_inc(s_hhi, 1)

            def side_work(u, t, g, name, tt):
                (kind, m), at = kind_no(name), side_bank(u, g, name)
                if kind == "mt":
                    max_rows(*next_job(u, t, g), at)
                elif kind == "xt":
                    act.wait_ge(s_xt_ps, KC * tt + m + 1)
                    nc.scalar.copy(aT[0][:, m, :], side_ps[at][:, :]).then_inc(s_xhi, 1)
                elif kind == "yt":
                    act.wait_ge(s_yt_ps, KC * tt + m + 1)
                    nc.scalar.copy(aT[0][:, m, :], side_ps[at][:, :]).then_inc(s_yhi, 1)
                elif kind in ("qs", "ks", "kx", "qx"):
                    high({"qs": QS, "ks": KS, "kx": KX, "qx": QX}[kind], m, tt, at)
                elif kind == "at":
                    if m == 0 and not is_at(tt, 0):
                        act.wait_ge(s_hlo, 2 * NHID * tt)
                    act.wait_ge(s_att_ps, KC * tt + m + 1)
                    nc.scalar.copy(oT[:, m, :], side_ps[at][:, :]).then_inc(s_att, 1)
                elif kind == "v":
                    act.wait_ge(s_v_ps, 2 * tt + m + 1)
                    nc.scalar.copy(V[S][:, 2 * m:2 * m + 2, :, 0:HD],
                                   side_ps[at][:, :].rearrange("p (c h d) -> p c h d", c=2, d=HD)).then_inc(s_v, 1)
                elif kind == "gu":
                    gate_tanh(tt, m, at)

            def side_work_after(u, t, g, name, tt):
                kind, m = kind_no(name)
                if kind == "mt":
                    max_rows_load(*next_job(u, t, g))
                elif kind == "gu":
                    hidden_high(tt, m)

            def attention(u, t, trailing):
                for g in range(NG):
                    for kt in range(NT):
                        wd = width(u, kt)
                        before = NT * job(u, t, g) + kt - 1
                        if not (isinstance(before, int) and before <= 0):
                            act.wait_ge(s_pv, before)
                        for end, cs in enumerate(halves(u, kt)):
                            for c, heads in cs:
                                act.wait_ge(s_score, exp_no(u, t, g, c) + 1)
                                src = score_ps[score_bank(u, g, c)][:, 0:wd * len(heads)].rearrange("p (h c) -> p h c", c=wd)
                                nc.scalar.activation(P[kt % 2][:, heads[0]:heads[-1] + 1, 0:wd], src, ACT.Exp).then_inc(s_exp, 1)
                            for name, gg in beside(u, t, g, kt, end, back=1):
                                side_work_after(u, t, gg, name, sequence(u, name, t))
                            if trailing and kt == 0 and end:
                                pv_out(*trailing)
                            for name, _ in beside(u, t, g, kt, end):
                                side_work(u, t, g, name, sequence(u, name, t))
                    trailing = (u, t, g)
                for name, g in beside(u, t, NG - 1, NT - 1, 1):
                    side_work_after(u, t, g, name, sequence(u, name, t))
                return trailing

            def first_rows(u, t, g, at):
                max_rows(u, t, g, at)
                max_rows_load(u, t, g)

            for name in BEFORE_FIRST:
                side_work(X, -2, 0, name, 0)
            first_rows(S, 0, 0, 0)
            act.wait_ge(s_w_set, 5)
            trailing = attention(S, 0, None)
            pv_out(*trailing)
            for n, name in enumerate(AFTER_FIRST):
                side_work(X, -1, 0, name, sequence(X, name, -1))
                if n == MAXIMA_0_LOADED:
                    first_rows(S, 1, 0, 0)
            attention(S, 1, None)
            with act.Fori(0, LAST - 1) as t:
                trailing = attention(X, t, (S, t + 1, NG - 1))
                attention(S, t + 2, trailing)
            trailing = attention(X, LAST - 1, (S, LAST, NG - 1))
            pv_out(*trailing)
            first_rows(X, LAST, 0, 1)
            for name in BEFORE_FINAL:
                side_work(S, LAST + 1, 0, name, LAST - 1)
            for name in BEFORE_FINAL:
                side_work_after(S, LAST + 1, 0, name, LAST - 1)
            trailing = attention(X, LAST, None)
            pv_out(*trailing)
            for n, name in enumerate(AFTER_FINAL):
                side_work(S, LAST + 2, 0, name, LAST)
                if n:
                    side_work_after(S, LAST + 2, 0, AFTER_FINAL[n - 1], LAST)

        @block.vector
        def _(dve):
            def norm(i, src, t, tiles=range(NT)):
                for c in tiles:
                    nc.vector.bn_stats(stats[:, c, :], src[:, c, :]).then_inc(s_stat[i], 1)
                if tiles[-1] == NT - 1:
                    for c in range(NT):
                        wait_apart(dve, s_stat[i], NT * t + c + 1)
                        nc.vector.bn_aggr(mv[:, c, :], stats[:, c, :]).then_inc(s_aggr[i], 1)

            def norm_end(i, src, t, tiles=range(NT)):
                if tiles[0] == 0:
                    dve.wait_ge(s_rstd[i], t + 1)
                for c in tiles:
                    rows, to = src[:, c, :], ln[:, c, :]
                    if i == 1:
                        rows, to = rows.rearrange("p (m h d) -> p m d h", m=2, d=HD), to.rearrange("p (m d h) -> p m d h", m=2, d=HD)
                    nc.vector.tensor_scalar(to, rows, mv[:, c, 0:1], rstd[:, c:c + 1], ALU.subtract, ALU.mult).then_inc(s_ln[i], 1)

            def take_max(u, t, g, i):
                keys = 128 * (i % NT + 1) if u == S else T
                dve.wait_ge(s_max_ps, max_no(u, t, g, i) + 1)
                nc.vector.tensor_reduce(mx[g % 2][:, i % NT, i // NT:i // NT + 1], max_ps[max_bank(g, i)][:, 0:keys], AX.X,
                                        ALU.max, negate=True).then_inc(s_max, 1)

            def low(m, t, at, sem_hi, sem_lo):
                dve.wait_ge(sem_hi, KC * t + m + 1)
                nc.vector.tensor_tensor(aT[1][:, m, :], side_ps[at][:, :], aT[0][:, m, :].bitcast(f32), ALU.subtract).then_inc(sem_lo, 1)

            def left_over(w, m, t, at):
                n, b = split_no(w, m, t), SPLIT_PLACE[w, m] % 2
                dve.wait_ge(s_hi, n + 1)
                nc.vector.scalar_tensor_tensor(rest[b][:, :], side_ps[at][:, :], SCALE if w in (QS, QX) else 1.0,
                                               parts[b][:, part_place(w, 0), :], ALU.mult, ALU.subtract).then_inc(s_rest, 1)
                if isinstance(t, int):
                    dve.wait_ge(s_rest, n + 1)
                    nc.vector.tensor_copy(parts[b][:, part_place(w, 1), :], rest[b][:, :]).then_inc(s_mid, 1)

            def head_outputs(u, t, g, at):
                j = job(u, t, g)
                dve.wait_ge(s_ot_ps, j + 1)
                src = side_ps[at][:, :].rearrange("p (c h e) -> p c h e", c=NT, h=GH)
                nc.vector.reciprocal(rden[g % 2][:, :, :], src[:, :, :, HD]).then_inc(s_rden, 1)
                dve.wait_ge(s_rden, j + 1)
                to = att[:, :, HD * GH * g:HD * GH * (g + 1)].rearrange("p c (h d) -> p c h d", d=HD)
                nc.vector.tensor_tensor(to, src[:, :, :, 0:HD], rden[g % 2][:, :, :].unsqueeze(3).broadcast_to([128, NT, GH, HD]),
                                        ALU.mult).then_inc(s_ot, 1)

            def add_wo(t, half, at):
                dve.wait_ge(s_again, 16 * (t + 1))
                dve.wait_ge(s_wo_ps, 2 * t + half + 1)
                rows = x1[:, 2 * half:2 * half + 2, :]
                nc.vector.tensor_tensor(rows, side_ps[at][:, :].rearrange("p (c d) -> p c d", c=2), rows, ALU.add).then_inc(s_x1, 1)

            def add_att(t):
                dve.wait_ge(s_ot, job(X, t, NG - 1) + 1)
                if not is_at(t, LAST):
                    dve.wait_ge(s_moved, t + 1)
                nc.vector.tensor_tensor(result(t)[:, :, :], result(t)[:, :, :], att[:, :, :], ALU.add).then_inc(s_x2, 1)

            def hidden(t, k, at):
                n = 2 * NHID * t + k
                dve.wait_ge(s_hlo, 2 * NHID + n - 1)
                dve.wait_ge(s_tanh, n + 1)
                nc.vector.scalar_tensor_tensor(gate[k % 2], gate[k % 2], 1.0, side_ps[at][:, 0:T // 2],
                                               ALU.add, ALU.mult).then_inc(s_gate, 1)
                dve.wait_ge(s_gate, n + 1)
                nc.vector.tensor_tensor(hid32[k % 2], side_ps[at][:, T // 2:T], gate[k % 2], ALU.mult).then_inc(s_hid, 1)

            def output(t, r, at):
                dve.wait_ge(s_dn_ps, NT * t + r + 1)
                rows = result(t)[:, r, :]
                nc.vector.scalar_tensor_tensor(rows, side_ps[at][:, 0:D], W_SCALE ** 3 / 2, rows,
                                               ALU.mult, ALU.add).then_inc(s_y, 1)

            def side_work(u, t, g, name, tt):
                (kind, m), at = kind_no(name), side_bank(u, g, name)
                if kind == "ot":
                    head_outputs(*prev_job(u, t, g), at)
                elif kind in ("qs", "ks", "kx", "qx"):
                    left_over({"qs": QS, "ks": KS, "kx": KX, "qx": QX}[kind], m, tt, at)
                elif kind == "xt":
                    low(m, tt, at, s_xhi, s_xt)
                elif kind == "yt":
                    low(m, tt, at, s_yhi, s_yt)
                elif kind == "wo":
                    add_wo(tt, m, at)
                elif kind == "gu":
                    hidden(tt, m, at)
                elif kind == "dn":
                    output(tt, m, at)

            FFN_WEIGHTS_AT = [(S, 2, 2, 1), (S, 2, 3, 1)]

            def norm_step(u, t, g, kt, end):
                place, low_rows, high_rows = (u, g, kt, end), range(NT // 2), range(NT // 2, NT)
                if u == X and not (isinstance(t, int) and t >= LAST - 1):
                    if place == (X, 0, 0, 0):
                        dve.wait_ge(s_x, 16 * (t + 3))
                        norm(0, x_in, t + 2, low_rows)
                    elif place == (X, 0, 0, 1):
                        norm(0, x_in, t + 2, high_rows)
                    elif place == (X, 0, 1, 1):
                        dve.wait_ge(s_hlo, 2 * NHID * (t + 1))
                        norm_end(0, x_in, t + 2, low_rows)
                    elif place == (X, 0, 2, 0):
                        norm_end(0, x_in, t + 2, high_rows)
                if u == X and is_at(t, LAST - 1):
                    if place == (X, 1, 0, 0):
                        dve.wait_ge(s_x1, 2 * (t + 2))
                        norm(1, x1, t + 1, low_rows)
                    elif place == (X, 1, 0, 1):
                        norm(1, x1, t + 1, high_rows)
                    elif place == (X, 1, 1, 1):
                        norm_end(1, x1, t + 1, low_rows)
                    elif place == (X, 1, 2, 0):
                        norm_end(1, x1, t + 1, high_rows)
                elif u == X and not is_at(t, LAST):
                    if place == (X, 1, 3, 0):
                        dve.wait_ge(s_x1, 2 * (t + 2))
                        norm(1, x1, t + 1, low_rows)
                    elif place == (X, 1, 3, 1):
                        norm(1, x1, t + 1, high_rows)
                    elif place == (X, 2, 0, 1):
                        norm_end(1, x1, t + 1, low_rows)
                    elif place == (X, 2, 1, 0):
                        norm_end(1, x1, t + 1, high_rows)
                if u == S and not (isinstance(t, int) and t <= 1):
                    if place == (S, 0, 2, 0):
                        add_att(t - 2)
                    elif place == (S, 0, 2, 1):
                        dve.wait_ge(s_x2, t - 1)
                        norm(2, result(t - 2), t - 2, low_rows)
                    elif place == (S, 0, 3, 0):
                        norm(2, result(t - 2), t - 2, high_rows)
                    elif place == (S, 0, 3, 1):
                        norm_end(2, result(t - 2), t - 2, low_rows)
                    elif place == (S, 1, 0, 0):
                        norm_end(2, result(t - 2), t - 2, high_rows)
                if u == S and is_at(t, 0):
                    if place == (S, 1, 0, 1):
                        dve.wait_ge(s_x, 16 * 2)
                        norm(0, x_in, 1)
                    elif place == (S, 1, 2, 1):
                        norm_end(0, x_in, 1)
                    elif place in FFN_WEIGHTS_AT:
                        n = FFN_WEIGHTS_AT.index(place)
                        split_weights(5 + n, *((wd_in[0], Wd, 0, NT), (wd_in[1], Wd, NT, NHID))[n])
                    elif place == (S, 3, 0, 1):
                        dve.wait_ge(s_w_set, 7)
                        for i, w_sb in enumerate((Wg, Wu, Wd)):
                            nc.vector.tensor_reduce(low_max[:, i:i + 1], w_sb[1][:, :, :].bitcast(f32), AX.XY, ALU.max,
                                                    apply_absolute_value=True).then_inc(s_low, 1)
                        dve.wait_ge(s_low, 3)
                        nc.vector.tensor_reduce(low_max[:, 3:4], low_max[:, 0:3], AX.X, ALU.max).then_inc(s_low, 1)

            def cross_out(t):
                add_att(t)
                dve.wait_ge(s_x2, t + 1)
                norm(2, result(t), t)

            def attention(u, t):
                for g in range(NG):
                    ahead = max_job(u, t, g)
                    for kt in range(NT):
                        for end in range(2):
                            for name, gg in beside(u, t, g, kt, end, back=1):
                                side_work(u, t, gg, name, sequence(u, name, t))
                            if ahead:
                                take_max(*ahead, 4 * kt + 2 * end)
                                take_max(*ahead, 4 * kt + 2 * end + 1)
                            norm_step(u, t, g, kt, end)
                for name, g in beside(u, t, NG - 1, NT - 1, 1):
                    side_work(u, t, g, name, sequence(u, name, t))

            def split_weights(n, w_in, w_sb, k0, k1):
                nc.vector.tensor_copy(w_sb[0][:, k0:k1, :], w_in).then_inc(s_whi, 1)
                dve.wait_ge(s_whi, n + 1)
                nc.vector.tensor_tensor(w_sb[1][:, k0:k1, :], w_in, w_sb[0][:, k0:k1, :].bitcast(f32),
                                        ALU.subtract).then_inc(s_w_set, 1)

            dve.sem_inc(s_y, NT)
            dve.sem_inc(s_out, 16)

            dve.wait_ge(s_x, 16)
            norm(0, x_in, 0)
            dve.wait_ge(s_w, 16 * 4)
            split_weights(0, wq_in, Wq, 0, KC)
            norm_end(0, x_in, 0)
            split_weights(1, wk_in, Wk, 0, KC)
            for name in BEFORE_FIRST:
                if name == "qs0":
                    split_weights(2, wv_in, Wv, 0, KC)
                if name == "v0":
                    dve.wait_ge(s_wi, 16 * 4)
                    split_weights(3, wg_in, Wg, 0, KC)
                    split_weights(4, wu_in, Wu, 0, KC)
                side_work(X, -2, 0, name, 0)
            for g in range(2):
                for i in range(GH * NT):
                    take_max(S, 0, g, i)
            attention(S, 0)
            head_outputs(S, 0, NG - 1, 0)
            dve.wait_ge(s_low_ps, 1)
            nc.vector.tensor_reduce(low_any[:, :], side_ps[1][0:1, 0:128], AX.X, ALU.max).then_inc(s_low, 1)
            dve.wait_ge(s_low, 5)
            nc.vector.tensor_scalar(low_flag[:, :], low_any[:, :], 0.0, None, ALU.not_equal).then_inc(s_low, 1)
            for n, name in enumerate(AFTER_FIRST):
                if name == "v0":
                    norm_end(1, x1, 0)
                side_work(X, -1, 0, name, sequence(X, name, -1))
                for i in range(PER_ITEM * n, min(PER_ITEM * (n + 1), 2 * GH * NT)):
                    take_max(S, 1, i // (GH * NT), i % (GH * NT))
                if name == "wo1":
                    dve.wait_ge(s_x1, 2)
                    norm(1, x1, 0)
            attention(S, 1)
            with dve.Fori(0, LAST - 1) as t:
                attention(X, t)
                attention(S, t + 2)
            attention(X, LAST - 1)
            head_outputs(X, LAST - 1, NG - 1, 0)
            cross_out(LAST - 1)
            for i in range(FINAL_MAXIMA[0]):
                take_max(X, LAST, 1, i)
            norm_end(2, x2, LAST - 1)
            for n, name in enumerate(BEFORE_FINAL):
                side_work(S, LAST + 1, 0, name, LAST - 1)
                for i in range(FINAL_MAXIMA[n], FINAL_MAXIMA[n + 1]):
                    take_max(X, LAST, 1, i)
            attention(X, LAST)
            head_outputs(X, LAST, NG - 1, 0)
            cross_out(LAST)
            dve.wait_ge(s_hlo, 2 * NHID * B)
            norm_end(2, x1, LAST)
            for name in AFTER_FINAL:
                side_work(S, LAST + 2, 0, name, LAST)



def kernel(**inputs):
    import numpy as np
    import ml_dtypes
    import concourse.bacc as bacc
    from concourse.bass_utils import run_bass_kernel_spmd as run

    bf = ml_dtypes.bfloat16
    a = {k: np.asarray(v) for k, v in inputs.items()}
    B, T, D = a["x"].shape
    NH = 16

    def three_parts(v):
        parts = []
        for _ in range(3):
            parts.append(v.astype(bf))
            v = v - parts[-1].astype(np.float64)
        return np.stack(parts)

    base = 2.0 ** (-8.0 / NH)
    slopes = np.array([base ** i for i in range(1, NH + 1)], np.float32).astype(np.float64)
    ramp = three_parts(slopes[:, None] * np.arange(T))
    ramp = np.stack([ramp, np.zeros_like(ramp)])
    fill = np.ones((3, NH, T), bf)
    at = np.arange(128)
    hidden = np.where(at[:, None] < at[None, :], -1e30, 0.0)
    masks = np.stack([hidden, hidden.T, np.eye(128)], 1).astype(bf)

    def by_channel(v):
        return v.reshape(*v.shape[:-1], 2, NH // 2, D // NH).swapaxes(-1, -2).reshape(v.shape)

    arrays = {
        "x": a["x"], "ctx": by_channel(a["ctx_1024"]),
        "wq": by_channel(a["L0_attn_Wq"].T), "wk": by_channel(a["L0_attn_Wk"].T), "wv": a["L0_attn_Wv"].T, "wo": a["L0_attn_Wo"].T,
        "w_gate": a["L0_ffn_w_gate"].T, "w_up": a["L0_ffn_w_up"].T, "w_down": a["L0_ffn_w_down"].T,
        "ramp": ramp, "fill": fill, "masks": masks,
    }
    arrays = {f"{k}_dram": np.ascontiguousarray(v) for k, v in arrays.items()}
    nc = bacc.Bacc("TRN2", target_bir_lowering=False, num_devices=1)
    ins = [nc.dram_tensor(k, v.shape, mybir.dt.from_np(v.dtype), kind="ExternalInput").ap() for k, v in arrays.items()]
    parts = nc.dram_tensor("parts_dram", (4, 2, 3, 128, T), mybir.dt.bfloat16, kind="Internal").ap()
    out = nc.dram_tensor("out_dram", (B, T, D), mybir.dt.float32, kind="ExternalOutput").ap()
    decoder_kernel(nc, *ins, parts, out)
    r = run(nc, [arrays], core_ids=[0])
    return r.results[0]["out_dram"]
```
